# Optimizing a Trainium2 kernel written in Bass

```python
import numpy as np
import jax
import jax.numpy as jnp

def _softmax(x, axis=-1):
    return jax.nn.softmax(x, axis=axis)

def _gelu(x):
    return jax.nn.gelu(x, approximate=True)

def _silu(x):
    return jax.nn.silu(x)

def _sigmoid(x):
    return jax.nn.sigmoid(x)

def _layernorm(x, axis=-1, eps=1e-05):
    m = jnp.mean(x, axis=axis, keepdims=True)
    v = jnp.var(x, axis=axis, keepdims=True)
    return (x - m) / jnp.sqrt(v + eps)

def _scatter_add(tgt, idx, src, axis=0):
    return tgt.at[idx].add(src)

def _segment_sum(src, seg, n):
    return jax.ops.segment_sum(src, seg, n)
kernel_name = 'mk_sandwich_d1_jaxref_r4_2ba063'

def setup_inputs(seed: int=0):
    np.random.seed(seed)
    _w = jnp.asarray

    def _L0_attn_setup():
        import jax, jax.numpy as jnp
        import numpy as np
        N_HEAD = 16
        PAGE_SIZE = 64
        ROPE_THETA = 10000.0

        def _rope_tables(T, D, dtype):
            inv = 1.0 / ROPE_THETA ** (np.arange(0, D, 2, dtype=np.float32) / D)
            ang = np.outer(np.arange(T, dtype=np.float32), inv)
            return (jnp.asarray(np.cos(ang), dtype), jnp.asarray(np.sin(ang), dtype))

        def _apply_rope(x, cos, sin):
            x1 = x[..., 0::2]
            x2 = x[..., 1::2]
            c = cos[None, :, None, :]
            s = sin[None, :, None, :]
            out = jnp.stack([x1 * c - x2 * s, x1 * s + x2 * c], axis=-1)
            return out.reshape(x.shape)
        key = jax.random.key(seed)
        ks = jax.random.split(key, 6)
        B, T, E = (2, 512, 256)
        L = E // 2
        sc = lambda fan: 1.0 / np.sqrt(fan)
        return {'x': jax.random.normal(ks[0], (B, T, E), jnp.float32), 'wq': jax.random.normal(ks[1], (E, E), jnp.float32) * sc(E), 'w_down': jax.random.normal(ks[2], (E, L), jnp.float32) * sc(E), 'wk_up': jax.random.normal(ks[3], (L, E), jnp.float32) * sc(L), 'wv_up': jax.random.normal(ks[4], (L, E), jnp.float32) * sc(L), 'wo': jax.random.normal(ks[5], (E, E), jnp.float32) * sc(E)}
    _L0_attn_in = _L0_attn_setup()

    def _L0_ffn_setup():
        import jax, jax.numpy as jnp
        import numpy as np
        D_IN, D_HID = (256, 1024)

        def _ternary(key, shape):
            return jax.random.randint(key, shape, -1, 2).astype(jnp.float32)

        def _tlin(x, w, s):
            return jnp.einsum('bsi,oi->bso', x, w) * s
        key = jax.random.key(seed)
        ks = jax.random.split(key, 12)
        inv = lambda fan: 1.0 / np.sqrt(fan).astype(np.float32)
        return {'x': jax.random.normal(ks[0], (4, 512, D_IN), dtype=jnp.float32), 'w1_w': _ternary(ks[1], (D_HID, D_IN)), 'w1_s': jax.random.uniform(ks[2], (D_HID,), dtype=jnp.float32) * inv(D_IN), 'w2_w': _ternary(ks[3], (D_HID, D_IN)), 'w2_s': jax.random.uniform(ks[4], (D_HID,), dtype=jnp.float32) * inv(D_IN), 'h1_w': _ternary(ks[5], (D_HID, D_HID)), 'h1_s': jax.random.uniform(ks[6], (D_HID,), dtype=jnp.float32) * inv(D_HID), 'h2_w': _ternary(ks[7], (D_HID, D_HID)), 'h2_s': jax.random.uniform(ks[8], (D_HID,), dtype=jnp.float32) * inv(D_HID), 'w3_w': _ternary(ks[9], (D_IN, D_HID)), 'w3_s': jax.random.uniform(ks[10], (D_IN,), dtype=jnp.float32) * inv(D_HID)}
    _L0_ffn_in = _L0_ffn_setup()
    _d = {'L0_attn_x': _L0_attn_in['x'], 'L0_attn_wq': _L0_attn_in['wq'], 'L0_attn_w_down': _L0_attn_in['w_down'], 'L0_attn_wk_up': _L0_attn_in['wk_up'], 'L0_attn_wv_up': _L0_attn_in['wv_up'], 'L0_attn_wo': _L0_attn_in['wo'], 'L0_ffn_w1_w': _L0_ffn_in['w1_w'], 'L0_ffn_w1_s': _L0_ffn_in['w1_s'], 'L0_ffn_w2_w': _L0_ffn_in['w2_w'], 'L0_ffn_w2_s': _L0_ffn_in['w2_s'], 'L0_ffn_h1_w': _L0_ffn_in['h1_w'], 'L0_ffn_h1_s': _L0_ffn_in['h1_s'], 'L0_ffn_h2_w': _L0_ffn_in['h2_w'], 'L0_ffn_h2_s': _L0_ffn_in['h2_s'], 'L0_ffn_w3_w': _L0_ffn_in['w3_w'], 'L0_ffn_w3_s': _L0_ffn_in['w3_s']}
    _x0 = _d['L0_attn_x']
    _d['L0_attn_x'] = jax.random.normal(jax.random.fold_in(jax.random.key(seed), 1), (16, 512, 256), dtype=_x0.dtype)
    del _x0
    return _d

def reference(L0_attn_x, L0_attn_wq, L0_attn_w_down, L0_attn_wk_up, L0_attn_wv_up, L0_attn_wo, L0_ffn_w1_w, L0_ffn_w1_s, L0_ffn_w2_w, L0_ffn_w2_s, L0_ffn_h1_w, L0_ffn_h1_s, L0_ffn_h2_w, L0_ffn_h2_s, L0_ffn_w3_w, L0_ffn_w3_s):

    def _L0_attn_ref(x, wq, w_down, wk_up, wv_up, wo):
        import jax, jax.numpy as jnp
        import numpy as np
        N_HEAD = 16
        PAGE_SIZE = 64
        ROPE_THETA = 10000.0

        def _rope_tables(T, D, dtype):
            inv = 1.0 / ROPE_THETA ** (np.arange(0, D, 2, dtype=np.float32) / D)
            ang = np.outer(np.arange(T, dtype=np.float32), inv)
            return (jnp.asarray(np.cos(ang), dtype), jnp.asarray(np.sin(ang), dtype))

        def _apply_rope(x, cos, sin):
            x1 = x[..., 0::2]
            x2 = x[..., 1::2]
            c = cos[None, :, None, :]
            s = sin[None, :, None, :]
            out = jnp.stack([x1 * c - x2 * s, x1 * s + x2 * c], axis=-1)
            return out.reshape(x.shape)
        B, T, E = x.shape
        H = N_HEAD
        D = E // H
        q = (x @ wq).reshape(B, T, H, D)
        lat = x @ w_down
        k = (lat @ wk_up).reshape(B, T, H, D)
        v = (lat @ wv_up).reshape(B, T, H, D)
        cos, sin = _rope_tables(T, D, x.dtype)
        q = _apply_rope(q, cos, sin)
        k = _apply_rope(k, cos, sin)
        scale = 1.0 / jnp.sqrt(jnp.asarray(D, x.dtype))
        scores = jnp.einsum('bqhd,bkhd->bhqk', q, k) * scale
        pages = jnp.arange(T) // PAGE_SIZE
        allowed = pages[None, :] <= pages[:, None]
        scores = jnp.where(allowed[None, None], scores, jnp.finfo(scores.dtype).min)
        attn = jax.nn.softmax(scores, axis=-1)
        out = jnp.einsum('bhqk,bkhd->bqhd', attn, v).reshape(B, T, E)
        return out @ wo

    def _L0_ffn_ref(x, w1_w, w1_s, w2_w, w2_s, h1_w, h1_s, h2_w, h2_s, w3_w, w3_s):
        import jax, jax.numpy as jnp
        import numpy as np
        D_IN, D_HID = (256, 1024)

        def _ternary(key, shape):
            return jax.random.randint(key, shape, -1, 2).astype(jnp.float32)

        def _tlin(x, w, s):
            return jnp.einsum('bsi,oi->bso', x, w) * s
        h = jax.nn.silu(_tlin(x, w1_w, w1_s)) * _tlin(x, w2_w, w2_s)
        h = jax.nn.gelu(_tlin(h, h1_w, h1_s), approximate=False)
        h = jax.nn.gelu(_tlin(h, h2_w, h2_s), approximate=False)
        return _tlin(h, w3_w, w3_s)
    x = L0_attn_x
    x = x + _layernorm(_L0_attn_ref(_layernorm(x, axis=-1), L0_attn_wq, L0_attn_w_down, L0_attn_wk_up, L0_attn_wv_up, L0_attn_wo), axis=-1)
    x = x + _layernorm(_L0_ffn_ref(_layernorm(x, axis=-1), L0_ffn_w1_w, L0_ffn_w1_s, L0_ffn_w2_w, L0_ffn_w2_s, L0_ffn_h1_w, L0_ffn_h1_s, L0_ffn_h2_w, L0_ffn_h2_s, L0_ffn_w3_w, L0_ffn_w3_s), axis=-1)
    return x

_drawn_inputs = setup_inputs


def setup_inputs(seed=0):
    import zlib

    import numpy as np

    out = dict(_drawn_inputs(seed))
    spreads = {}
    factors = {}
    for name, (base, spread) in spreads.items():
        noise = np.random.default_rng([zlib.crc32(name.encode()), seed]).standard_normal(out[name].shape)
        drawn = base * np.exp(spread * noise) if base else spread * noise
        out[name] = jnp.asarray(drawn.astype(out[name].dtype))
    for name, factor in factors.items():
        out[name] = (out[name] * factor).astype(out[name].dtype)
    return out
```

```python
from contextlib import ExitStack

import numpy as np

import concourse.bass as bass
from concourse import mybir

F32 = mybir.dt.float32
BF16 = mybir.dt.bfloat16
ALU = mybir.AluOpType
ACT = mybir.ActivationFunctionType
AX = mybir.AxisListType

P = 128
B, T, E = 16, 512, 256
L = E // 2
H, D = 16, 16
F = 1024
PAGE = 64
TT = T // P
KE = E // P
KF = F // P
HG = 4
NG = H // HG
VW = D + 1
COL = 32
EPS = 1e-5
SCALE = float(D) ** -0.5
MASKED = -1e30
ROWS_QK = 7 * D
ROW_MASK = ROWS_QK
ROW_MAX = ROW_MASK + TT
Q_STACK = ((0, 0, 1), (0, 1, 1), (0, 2, 1), (1, 3, 1), (1, 4, 1), (1, 5, 1), (2, 6, 1))
K_STACK = ((0, 0, 3), (0, 3, 3), (0, 6, 1))
STACKS = 16 * (len(Q_STACK) + len(K_STACK))
WEIGHT_LOADS = 11
LN = TT + 7
STEPS = NG * TT


def program(nc, x, wq, wd, wk, wv, wo, w1, s1, w2, s2, h1, sh1, h2, sh2, w3, s3,
            cos, sin, qconst, kconst, ident, identb, out):
    scratch = nc.dram_tensor("qk_parts", [2, 3, 2, P, T], BF16).ap()
    max_scratch = nc.dram_tensor("max_parts", [3 * H, T], BF16).ap()
    with ExitStack() as ctx:
        def sb(name, shape, dt=F32):
            return ctx.enter_context(nc.sbuf_tensor(name, shape, dt))

        def sem(name):
            return ctx.enter_context(nc.semaphore(name))

        w1_sb, w2_sb = sb("w1_sb", [P, KE, F]), sb("w2_sb", [P, KE, F])
        h1_sb, h2_sb = sb("h1_sb", [P, KF, F]), sb("h2_sb", [P, KF, F])
        w3_sb = sb("w3_sb", [P, KF, E])
        wq_sb, wo_sb = sb("wq_sb", [P, KE, E]), sb("wo_sb", [P, KE, E])
        wd_sb = sb("wd_sb", [P, KE, L])
        wk_sb, wv_sb = sb("wk_sb", [P, E]), sb("wv_sb", [P, E])
        cos_sb, sin_sb = sb("cos_sb", [P, T]), sb("sin_sb", [P, T])
        s_sb = sb("s_sb", [P, 4, KF])
        s3_sb = sb("s3_sb", [P, E])
        id_sb, idb_sb = sb("id_sb", [P, P]), sb("idb_sb", [P, P], BF16)
        half = sb("half", [P, TT])

        qs, ks = sb("qs", [P, H, T], BF16), sb("ks", [P, H, T], BF16)
        v_sb = sb("v_sb", [P, TT, H, VW])
        rot = sb("rot", [P, 2, 2, T])
        parts = sb("parts", [P, 2, 3, T], BF16)
        mx, mr = sb("mx", [P, TT, H]), sb("mr", [P, TT, H])
        ms = sb("ms", [P, TT, 8, H], BF16)
        rsum = sb("rsum", [P, TT, HG])
        on = sb("on", [P, TT, E])
        x1n, x1o = sb("x1n", [P, TT, E]), sb("x1o", [P, TT, E])
        turned = sb("turned", [P, KE, T])
        hid_a, hid_b = sb("hid_a", [P, KF, T]), sb("hid_b", [P, KF, T])
        probs = hid_b[:, :, :].rearrange("p (s h) t -> p s h t", s=2)
        tmp = sb("tmp", [P, 2, T])
        xt = hid_a[:, 0:TT * E // T, :].rearrange("p a (b e) -> p (a b) e", e=E)
        og = rot[:, 1, 1, :]
        mt = parts[0:3 * H, 0, 0, :]
        xnT = rot[:, 0, :, :]
        latT = rot[:, 1, 0, :]
        stage = tmp[:, :, :].rearrange("p a (b e) -> p (a b) e", e=E)
        st = [sb(f"st{n}", [P, TT, 6]) for n in range(4)]
        mv = [sb(f"mv{n}", [P, 3, TT]) for n in range(4)]
        rs = [sb(f"rs{n}", [P, TT]) for n in range(4)]

        ps = ctx.enter_context(nc.psum_tensor("ps", [P, 8, T], F32))
        ps_mt = ps[:, 4, :].bitcast(BF16)[:, 0:T]

        weights_in, wffn_in, const_in, pool_const = (sem(n) for n in
                                                     ("weights_in", "wffn_in", "const_in", "pool_const"))
        sums_clear, max_out = sem("sums_clear"), sem("max_out")
        scratch_in = [sem(f"scratch_in{n}") for n in range(2)]
        x_in, xr_in, stack_in, mrow_in, out_done = (
            sem(n) for n in ("x_in", "xr_in", "stack_in", "mrow_in", "out_done"))
        stats = [sem(f"stats{n}") for n in range(4)]
        rstd = [sem(f"rstd{n}") for n in range(4)]
        xn_ready, x1_kept, x1_part, x1_ready, xn2_ready, y_done, out_ready = (
            sem(n) for n in ("xn_ready", "x1_kept", "x1_part", "x1_ready", "xn2_ready", "y_done", "out_ready"))
        xT_ps, lat_ps, qk_ps, v_ps, xT_sb, lat_sb, v_sbs = (
            sem(n) for n in ("xT_ps", "lat_ps", "qk_ps", "v_ps", "xT_sb", "lat_sb", "v_sbs"))
        terms, rotated, high_done, rest_done, mid_done, parts_ready = (
            sem(n) for n in ("terms", "rotated", "high_done", "rest_done", "mid_done", "parts_ready"))
        mx_ps, mx_used, msplit, mT_ps, mT_sb = (
            sem(n) for n in ("mx_ps", "mx_used", "msplit", "mT_ps", "mT_sb"))
        st_ps, exp_done, av_done, o_sb, o_ps, r_done, on_done = (
            sem(n) for n in ("st_ps", "exp_done", "av_done", "o_sb", "o_ps", "r_done", "on_done"))
        onT_ps, onT_sb, wo_ps, x2T_ps, x2T_sb = (
            sem(n) for n in ("onT_ps", "onT_sb", "wo_ps", "x2T_ps", "x2T_sb"))
        l1_ps, silu_done, g1_done, l2_ps, g2_done, l3_ps, g3_done, w3_ps, w3_used = (
            sem(n) for n in ("l1_ps", "silu_done", "g1_done", "l2_ps", "g2_done", "l3_ps", "g3_done",
                             "w3_ps", "w3_used"))

        def schedule(eng, steps):
            steps(None, None, 0)
            steps(0, None, 1)
            steps(1, 0, 2)
            with eng.Fori(2, B - 1) as i:
                steps(i, i - 1, i + 1)
            steps(B - 1, B - 2, None)
            steps(None, B - 1, None)

        def later(b):
            return not (isinstance(b, int) and b == 0)

        block = ctx.enter_context(nc.Block())

        @block.sync
        def _(sp):
            def load_weights():
                for dst, src in ((wq_sb, wq), (wd_sb, wd), (wo_sb, wo)):
                    sp.dma_start(dst[:], src.rearrange("(k p) n -> p k n", p=P)).then_inc(weights_in, 16)
                for dst, src in ((wk_sb, wk), (wv_sb, wv), (cos_sb, cos), (sin_sb, sin)):
                    sp.dma_start(dst[:], src).then_inc(weights_in, 16)
                for dst, src in ((qs, qconst), (ks, kconst)):
                    sp.dma_start(dst[ROWS_QK:P, :, :],
                                 src.unsqueeze(1).to_broadcast([P - ROWS_QK, H, T])).then_inc(weights_in, 16)
                for dst, src in ((id_sb, ident), (idb_sb, identb)):
                    sp.dma_start(dst[:], src).then_inc(weights_in, 16)
                for n, s in enumerate((s1, s2, sh1, sh2)):
                    sp.dma_start(s_sb[:, n, :], s).then_inc(wffn_in, 16)
                sp.dma_start(s3_sb[:], s3.to_broadcast([P, E])).then_inc(wffn_in, 16)
                for dst, src in ((w1_sb, w1), (w2_sb, w2), (h1_sb, h1), (h2_sb, h2), (w3_sb, w3)):
                    sp.dma_start(dst[:], src.rearrange("(k p) n -> p k n", p=P)).then_inc(wffn_in, 16)

            def batch(dram, b):
                return dram[bass.ds(b, 1)].rearrange("a (t p) e -> p (a t) e", p=P)

            def load_x(b, f):
                if f is not None and later(f):
                    sp.wait_ge(w3_ps, TT * f)
                elif later(b):
                    sp.wait_ge(xT_ps, b)
                sp.dma_start(xt, batch(x, b)).then_inc(x_in, 16)

            def reload_x(b):
                if later(b):
                    sp.wait_ge(x1_kept, b)
                sp.dma_start(x1n[:], batch(x, b)).then_inc(xr_in, 16)

            def stacks(b):
                for n in range(4):
                    if n == 0 and later(b):
                        sp.wait_ge(stack_in, STACKS * b)
                    sp.wait_ge(parts_ready, 4 * b + n + 1)
                    sp.dma_start(scratch[n // 2, :, n % 2].rearrange("c p t -> p c t"),
                                 parts[:, n % 2]).then_inc(scratch_in[n % 2], 16)
                    if n % 2:
                        if n == 1 and later(b):
                            sp.wait_ge(av_done, STEPS * b)
                        for half_ in range(2):
                            sp.wait_ge(scratch_in[half_], 32 * b + 8 * (n + 1))
                        rows = scratch[n // 2].rearrange("c a (d h) t -> (c a d) (h t)", h=H)
                        for at, to, k in Q_STACK if n == 1 else K_STACK:
                            dst = (qs, ks)[n // 2][to * D:(to + k) * D].rearrange("p h t -> p (h t)")
                            sp.dma_start(dst, rows[at * D:(at + k) * D]).then_inc(stack_in, 16)

            def max_rows(b):
                sp.wait_ge(mT_sb, b + 1)
                sp.dma_start(max_scratch, mt).then_inc(max_out, 16)
                sp.wait_ge(max_out, 16 * (b + 1))
                sp.dma_start(qs[ROW_MAX:ROW_MAX + 3].rearrange("p h t -> p (h t)"),
                             max_scratch.rearrange("(r h) t -> r (h t)", h=H)).then_inc(mrow_in, 16)

            def store(b):
                sp.wait_ge(out_ready, b + 1)
                sp.dma_start(batch(out, b), stage).then_inc(out_done, 16)

            def steps(a, f, p):
                if p is not None:
                    load_x(p, f)
                    if not later(p):
                        load_weights()
                if a is not None:
                    reload_x(a)
                if p is not None:
                    stacks(p)
                    max_rows(p)
                if f is not None:
                    store(f)

            schedule(sp, steps)
            sp.wait_ge(out_done, 16 * B)

        @block.gpsimd
        def _(pool):
            def inverse_deviation(n, b):
                pool.wait_ge(stats[n], LN * (b + 1))
                nc.gpsimd.tensor_tensor(rs[n][:], mv[n][:, 2, :], half[:], ALU.pow).then_inc(rstd[n], 1)

            def split_rest(b, n):
                s = n % 2
                pool.wait_ge(high_done, 4 * b + n + 1)
                nc.gpsimd.tensor_tensor(rot[:, s, 1, :], rot[:, s, 0, :], parts[:, s, 0, :],
                                        ALU.subtract).then_inc(rest_done, 1)
                pool.wait_ge(rest_done, 4 * b + n + 1)
                pool.wait_ge(mid_done, 4 * b + n + 1)
                nc.gpsimd.tensor_tensor(parts[:, s, 2, :], rot[:, s, 1, :], parts[:, s, 1, :],
                                        ALU.subtract).then_inc(parts_ready, 1)

            def steps(a, f, p):
                if p is not None:
                    inverse_deviation(0, p)
                if p is not None:
                    for n in range(4):
                        split_rest(p, n)
                if a is not None:
                    inverse_deviation(1, a)
                    inverse_deviation(2, a)
                if f is not None:
                    inverse_deviation(3, f)

            nc.gpsimd.memset(half[:], -0.5).then_inc(pool_const, 1)
            nc.gpsimd.memset(v_sb[:], 1.0).then_inc(pool_const, 1)
            pool.wait_ge(pool_const, 1)
            schedule(pool, steps)

        @block.scalar
        def _(act):
            def evac_xT(b):
                act.wait_ge(xT_ps, b + 1)
                if later(b):
                    act.wait_ge(parts_ready, 4 * b)
                nc.scalar.copy(xnT, ps[:, 6:8, :]).then_inc(xT_sb, 1)

            def evac_lat(b):
                act.wait_ge(lat_ps, b + 1)
                nc.scalar.copy(latT, ps[:, 2, :]).then_inc(lat_sb, 1)

            def evac_v(b):
                act.wait_ge(v_ps, b + 1)
                if not later(b):
                    act.wait_ge(pool_const, 2)
                nc.scalar.copy(v_sb[:, :, :, 0:D],
                               ps[:, 0:2, :].rearrange("p a (b h d) -> p (a b) h d", b=2, d=D)).then_inc(v_sbs, 1)

            def split_high(b, n):
                s = n % 2
                act.wait_ge(rotated, 4 * b + n + 1)
                if n >= 2 or later(b):
                    act.wait_ge(scratch_in[s], 32 * b + 16 * (n // 2))
                nc.scalar.copy(parts[:, s, 0, :], rot[:, s, 0, :]).then_inc(high_done, 1)
                act.wait_ge(rest_done, 4 * b + n + 1)
                nc.scalar.copy(parts[:, s, 1, :], rot[:, s, 1, :]).then_inc(mid_done, 1)

            def keep_x1(b):
                act.wait_ge(x1_ready, b + 1)
                if later(b):
                    act.wait_ge(out_ready, b)
                nc.scalar.copy(x1o[:], x1n[:]).then_inc(x1_kept, 1)

            def exps(b):
                for u in range(2 * STEPS):
                    g, k = u // 2, u // 2 % TT
                    n = T - P * k
                    act.wait_ge(st_ps, 2 * STEPS * b + u + 1)
                    if g >= 2:
                        act.wait_ge(av_done, STEPS * b + g - 1)
                    elif later(b):
                        act.wait_ge(av_done, STEPS * b + g - 1)
                    two = slice(2 * (u % 2), 2 * (u % 2) + 2)
                    nc.scalar.activation(probs[:, g % 2, two, 0:n], ps[:, two, 0:n], ACT.Exp,
                                         scale=SCALE).then_inc(exp_done, 1)

            def evac_onT(b):
                act.wait_ge(onT_ps, b + 1)
                nc.scalar.copy(turned[:], ps[:, 4:6, :]).then_inc(onT_sb, 1)

            def evac_x2T(b):
                act.wait_ge(x2T_ps, b + 1)
                nc.scalar.copy(turned[:], ps[:, 4:6, :]).then_inc(x2T_sb, 1)

            def evac_mT(b):
                act.wait_ge(mT_ps, b + 1)
                if later(b):
                    act.wait_ge(mrow_in, 16 * b)
                nc.scalar.copy(mt, ps_mt[0:3 * H]).then_inc(mT_sb, 1)

            def silu(b, m):
                act.wait_ge(l1_ps, 8 * b + m + 1)
                if m < 2 and later(b):
                    act.wait_ge(out_done, 16 * b)
                elif m >= 2:
                    act.wait_ge(g1_done, 8 * b + m - 1)
                nc.scalar.activation(tmp[:, m % 2, :], ps[:, 2 * (m % 2), :], ACT.Silu,
                                     scale=s_sb[:, 0, m:m + 1]).then_inc(silu_done, 1)

            def gelu(b, m, ready, dst, n, done):
                act.wait_ge(ready, 8 * b + m + 1)
                nc.scalar.activation(dst[:, m, :], ps[:, m % 4, :], ACT.Gelu,
                                     scale=s_sb[:, n, m:m + 1]).then_inc(done, 1)

            def steps(a, f, p):
                if f is not None:
                    keep_x1(f)
                if a is not None:
                    exps(a)
                if p is not None:
                    evac_xT(p)
                    evac_lat(p)
                    evac_v(p)
                for m in range(KF):
                    if f is not None:
                        silu(f, m)
                    if p is not None and m % 2 == 1:
                        split_high(p, m // 2)
                if a is not None:
                    evac_onT(a)
                if f is not None:
                    for m in range(KF):
                        gelu(f, m, l2_ps, hid_b, 2, g2_done)
                if a is not None:
                    evac_x2T(a)
                if f is not None:
                    for m in range(KF):
                        gelu(f, m, l3_ps, hid_a, 3, g3_done)
                if p is not None:
                    evac_mT(p)

            act.wait_ge(wffn_in, 160)
            schedule(act, steps)

        @block.vector
        def _(dve):
            def mean_variance(n, b, tiles):
                for t in range(TT):
                    nc.vector.bn_stats(st[n][:, t, :], tiles(t)).then_inc(stats[n], 1)
                mean, square = st[n][:, :, 1::3], st[n][:, :, 2::3]
                dve.wait_ge(stats[n], LN * b + TT)
                nc.vector.tensor_tensor(mv[n][:, 0, :], mean[:, :, 0], mean[:, :, 1], ALU.add).then_inc(stats[n], 1)
                nc.vector.tensor_tensor(mv[n][:, 1, :], mean[:, :, 0], mean[:, :, 1], ALU.subtract).then_inc(stats[n], 1)
                nc.vector.tensor_tensor(mv[n][:, 2, :], square[:, :, 0], square[:, :, 1], ALU.add).then_inc(stats[n], 1)
                dve.wait_ge(stats[n], LN * b + TT + 3)
                nc.vector.tensor_scalar(mv[n][:, 0, :], mv[n][:, 0, :], 0.5, None, ALU.mult).then_inc(stats[n], 1)
                nc.vector.tensor_scalar(mv[n][:, 2, :], mv[n][:, 2, :], 1.0 / E, EPS, ALU.mult,
                                        ALU.add).then_inc(stats[n], 1)
                nc.vector.scalar_tensor_tensor(out=mv[n][:, 1, :], in0=mv[n][:, 1, :], scalar=0.25,
                                               in1=mv[n][:, 1, :], op0=ALU.mult, op1=ALU.mult).then_inc(stats[n], 1)
                dve.wait_ge(stats[n], LN * b + TT + 6)
                nc.vector.tensor_tensor(mv[n][:, 2, :], mv[n][:, 2, :], mv[n][:, 1, :], ALU.add).then_inc(stats[n], 1)

            def normalise(n, b, dst, tiles, done):
                dve.wait_ge(rstd[n], b + 1)
                for t in range(TT):
                    nc.vector.tensor_scalar(dst(t), tiles(t), mv[n][:, 0, t:t + 1], rs[n][:, t:t + 1],
                                            ALU.subtract, ALU.mult).then_inc(done, 1)

            def norm_x(b):
                dve.wait_ge(x_in, 16 * b + 16)
                mean_variance(0, b, lambda t: xt[:, t, :])
                normalise(0, b, lambda t: xt[:, t, :], lambda t: xt[:, t, :], xn_ready)

            def heads_out(b):
                for g in range(NG):
                    dve.wait_ge(av_done, STEPS * b + TT * (g + 1))
                    if g or later(b):
                        dve.wait_ge(o_ps, NG * b + g)
                    nc.vector.tensor_copy(og, ps[:, 4, :]).then_inc(o_sb, 1)
                    dve.wait_ge(o_ps, NG * b + g + 1)
                    if g or later(b):
                        dve.wait_ge(on_done, NG * b + g)
                    heads = ps[:, 5, :].rearrange("p (t h c) -> p t h c", t=TT, c=COL)
                    nc.vector.reciprocal(rsum[:], heads[:, :, :, D]).then_inc(r_done, 1)
                    dve.wait_ge(r_done, NG * b + g + 1)
                    if g == 0 and later(b):
                        dve.wait_ge(x2T_ps, b)
                    nc.vector.tensor_tensor(
                        on[:, :, g * HG * D:(g + 1) * HG * D].rearrange("p t (h d) -> p t h d", d=D),
                        heads[:, :, :, 0:D], rsum[:].unsqueeze(3).to_broadcast([P, TT, HG, D]),
                        ALU.mult).then_inc(on_done, 1)

            def rotate(b, n):
                s, bank = n % 2, 4 + 2 * (n // 2)
                dve.wait_ge(qk_ps, 2 * b + n // 2 + 1)
                if n == 0:
                    dve.wait_ge(v_ps, b + 1)
                if n >= 2:
                    dve.wait_ge(parts_ready, 4 * b + n - 1)
                first, second = ((cos_sb, sin_sb), (sin_sb, cos_sb))[n % 2]
                nc.vector.tensor_tensor(rot[:, s, 0, :], ps[:, bank, :], first[:], ALU.mult).then_inc(terms, 1)
                nc.vector.tensor_tensor(rot[:, s, 1, :], ps[:, bank + 1, :], second[:], ALU.mult).then_inc(terms, 1)
                dve.wait_ge(terms, 8 * b + 2 * n + 2)
                nc.vector.tensor_tensor(rot[:, s, 0, :], rot[:, s, 0, :], rot[:, s, 1, :],
                                        (ALU.subtract, ALU.add)[n % 2]).then_inc(rotated, 1)

            def gate(b, m):
                dve.wait_ge(silu_done, 8 * b + m + 1)
                nc.vector.scalar_tensor_tensor(out=hid_a[:, m, :], in0=ps[:, 2 * (m % 2) + 1, :],
                                               scalar=s_sb[:, 1, m:m + 1], in1=tmp[:, m % 2, :],
                                               op0=ALU.mult, op1=ALU.mult).then_inc(g1_done, 1)

            def attn_norms(b):
                dve.wait_ge(wo_ps, b + 1)
                proj = lambda t: ps[:, 6 + t // 2, (t % 2) * E:(t % 2 + 1) * E]
                mean_variance(1, b, proj)
                normalise(1, b, lambda t: on[:, t, :], proj, x1_part)
                dve.wait_ge(x1_part, TT * (b + 1))
                dve.wait_ge(xr_in, 16 * (b + 1))
                nc.vector.tensor_tensor(x1n[:], x1n[:], on[:], ALU.add).then_inc(x1_ready, 1)
                dve.wait_ge(x1_ready, b + 1)
                mean_variance(2, b, lambda t: x1n[:, t, :])
                normalise(2, b, lambda t: on[:, t, :], lambda t: x1n[:, t, :], xn2_ready)

            def head_max(b, h2, t):
                u = TT * h2 + t
                n = P * (t + 1)
                dve.wait_ge(mx_ps, 32 * b + u + 1)
                two = slice(4 + 2 * (u % 2), 6 + 2 * (u % 2))
                nc.vector.tensor_reduce(mx[:, t, 2 * h2:2 * h2 + 2], ps[:, two, 0:n], AX.X,
                                        ALU.max).then_inc(mx_used, 1)

            def split_max(b):
                dve.wait_ge(mx_used, 32 * (b + 1))
                nc.vector.tensor_scalar(ms[:, :, 0, :], mx[:], -1.0, None, ALU.mult).then_inc(msplit, 1)
                dve.wait_ge(msplit, 4 * b + 1)
                nc.vector.scalar_tensor_tensor(out=mr[:], in0=mx[:], scalar=-1.0, in1=ms[:, :, 0, :],
                                               op0=ALU.mult, op1=ALU.subtract).then_inc(msplit, 1)
                dve.wait_ge(msplit, 4 * b + 2)
                nc.vector.tensor_copy(ms[:, :, 1, :], mr[:]).then_inc(msplit, 1)
                dve.wait_ge(msplit, 4 * b + 3)
                nc.vector.tensor_tensor(ms[:, :, 2, :], mr[:], ms[:, :, 1, :], ALU.subtract).then_inc(msplit, 1)

            def ffn_norm(b):
                for t in range(TT):
                    dve.wait_ge(w3_ps, TT * b + t + 1)
                    nc.vector.tensor_tensor(stage[:, t, :], ps[:, t, 0:E], s3_sb[:], ALU.mult).then_inc(w3_used, 1)
                dve.wait_ge(w3_used, TT * (b + 1))
                mean_variance(3, b, lambda t: stage[:, t, :])
                normalise(3, b, lambda t: stage[:, t, :], lambda t: stage[:, t, :], y_done)
                dve.wait_ge(y_done, TT * (b + 1))
                dve.wait_ge(x1_kept, b + 1)
                nc.vector.tensor_tensor(stage, stage, x1o[:], ALU.add).then_inc(out_ready, 1)

            def steps(a, f, p):
                if p is not None:
                    norm_x(p)
                if a is not None:
                    heads_out(a)
                for m in range(KF):
                    if f is not None:
                        gate(f, m)
                    if p is not None and m % 2 == 1:
                        rotate(p, m // 2)
                if a is not None:
                    attn_norms(a)
                if p is not None:
                    for h2 in range(H // 2):
                        for t in range(TT):
                            head_max(p, h2, t)
                    split_max(p)
                if f is not None:
                    ffn_norm(f)

            nc.vector.memset(ps[:, 4, :], 0.0).then_inc(sums_clear, 1)
            nc.vector.memset(ms[:], 0.0).then_inc(sums_clear, 1)
            dve.wait_ge(sums_clear, 2)
            dve.wait_ge(weights_in, WEIGHT_LOADS * 16)
            dve.wait_ge(wffn_in, 160)
            schedule(dve, steps)

        @block.tensor
        def _(pe):
            def transposes(src, bank):
                for k in range(KE):
                    for t in range(TT):
                        last = nc.tensor.transpose(ps[:, bank + k, t * P:(t + 1) * P],
                                                   src[:, t, k * P:(k + 1) * P], id_sb[:])
                return last

            def project(b, a):
                pe.wait_ge(xn_ready, TT * (b + 1))
                transposes(xt, 6).then_inc(xT_ps, 1)
                pe.wait_ge(xT_sb, b + 1)
                for k in range(KE):
                    last = nc.tensor.matmul(ps[:, 2, :], wd_sb[:, k, :], xnT[:, k, :], start=(k == 0), stop=(k == KE - 1))
                last.then_inc(lat_ps, 1)
                if a is not None:
                    pe.wait_ge(on_done, NG * (a + 1))
                for half_ in range(2):
                    for k in range(KE):
                        last = nc.tensor.matmul(ps[:, 4 + half_, :], wq_sb[:, k, half_ * P:(half_ + 1) * P], xnT[:, k, :],
                                                start=(k == 0), stop=(k == KE - 1))
                last.then_inc(qk_ps, 1)
                pe.wait_ge(lat_sb, b + 1)
                for half_ in range(2):
                    last = nc.tensor.matmul(ps[:, 6 + half_, :], wk_sb[:, half_ * P:(half_ + 1) * P], latT,
                                            start=True, stop=True)
                last.then_inc(qk_ps, 1)
                for t in range(TT):
                    last = nc.tensor.matmul(ps[:, t // 2, (t % 2) * E:(t % 2 + 1) * E], latT[:, t * P:(t + 1) * P],
                                            wv_sb[:], start=True, stop=True)
                last.then_inc(v_ps, 1)

            def scores(b, gk):
                g, k = gk // TT, gk % TT
                n = T - P * k
                for two in range(2):
                    u = 2 * gk + two
                    if u >= 2 or later(b):
                        pe.wait_ge(exp_done, 2 * STEPS * b + u - 1)
                    for h in range(2):
                        head = g * HG + 2 * two + h
                        last = nc.tensor.matmul(ps[:, 2 * two + h, 0:n], ks[:, head, k * P:(k + 1) * P],
                                                qs[:, head, k * P:T], start=True, stop=True)
                    last.then_inc(st_ps, 1)

            def weigh(b, gk):
                g, k = gk // TT, gk % TT
                n = T - P * k
                pe.wait_ge(exp_done, 2 * (STEPS * b + gk + 1))
                if k == 0 and (g or later(b)):
                    pe.wait_ge(o_sb, NG * b + g)
                for h in range(HG):
                    last = nc.tensor.matmul(ps[h * COL:h * COL + VW, 4, k * P:T], v_sb[:, k, g * HG + h, :],
                                            probs[:, gk % 2, h, 0:n], start=(k == 0), stop=(k == TT - 1),
                                            skip_group_check=True)
                last.then_inc(av_done, 1)

            def turn_group(b, g):
                pe.wait_ge(o_sb, NG * b + g + 1)
                if g or later(b):
                    pe.wait_ge(on_done, NG * b + g)
                for t in range(TT):
                    last = nc.tensor.transpose(ps[:, 5, t * P:(t + 1) * P], og[:, t * P:(t + 1) * P], id_sb[:])
                last.then_inc(o_ps, 1)

            def attention(b, f_before):
                pe.wait_ge(stack_in, STACKS * (b + 1))
                pe.wait_ge(mrow_in, 16 * (b + 1))
                pe.wait_ge(v_sbs, b + 1)
                if f_before is not None and later(f_before):
                    pe.wait_ge(w3_used, TT * f_before)
                scores(b, 0)
                for gk in range(STEPS):
                    if gk + 1 < STEPS:
                        scores(b, gk + 1)
                    weigh(b, gk)
                    if gk % TT == 1 and gk > TT:
                        turn_group(b, gk // TT - 1)
                turn_group(b, NG - 1)

            def gated(b):
                pe.wait_ge(x2T_sb, b + 1)
                for m in range(KF):
                    if m >= 2:
                        pe.wait_ge(g1_done, 8 * b + m - 1)
                    for w, bank in ((w1_sb, 0), (w2_sb, 1)):
                        for k in range(KE):
                            last = nc.tensor.matmul(ps[:, 2 * (m % 2) + bank, :], w[:, k, m * P:(m + 1) * P],
                                                    turned[:, k, :], start=(k == 0), stop=(k == KE - 1))
                    last.then_inc(l1_ps, 1)

            def hidden(b, m, w, src, ready, own, done):
                pe.wait_ge(ready, 8 * (b + 1))
                if m >= 4:
                    pe.wait_ge(own, 8 * b + m - 3)
                for k in range(KF):
                    last = nc.tensor.matmul(ps[:, m % 4, :], w[:, k, m * P:(m + 1) * P], src[:, k, :],
                                            start=(k == 0), stop=(k == KF - 1))
                last.then_inc(done, 1)

            def output(b):
                pe.wait_ge(g3_done, 8 * (b + 1))
                for t in range(TT):
                    for k in range(KF):
                        last = nc.tensor.matmul(ps[:, t, 0:E], hid_a[:, k, t * P:(t + 1) * P], w3_sb[:, k, :],
                                                start=(k == 0), stop=(k == KF - 1))
                    last.then_inc(w3_ps, 1)

            def attn_out(b):
                pe.wait_ge(on_done, NG * (b + 1))
                transposes(on, 4).then_inc(onT_ps, 1)
                pe.wait_ge(onT_sb, b + 1)
                for t in range(TT):
                    for k in range(KE):
                        last = nc.tensor.matmul(ps[:, 6 + t // 2, (t % 2) * E:(t % 2 + 1) * E],
                                                turned[:, k, t * P:(t + 1) * P], wo_sb[:, k, :],
                                                start=(k == 0), stop=(k == KE - 1))
                last.then_inc(wo_ps, 1)

            def turn_x2(b):
                pe.wait_ge(xn2_ready, TT * (b + 1))
                transposes(on, 4).then_inc(x2T_ps, 1)

            def max_scores(b, h2):
                pe.wait_ge(stack_in, STACKS * (b + 1))
                for t in range(TT):
                    u = TT * h2 + t
                    n = P * (t + 1)
                    if u >= 2 or later(b):
                        pe.wait_ge(mx_used, 32 * b + u - 1)
                    for h in range(2):
                        head = 2 * h2 + h
                        last = nc.tensor.matmul(ps[:, 4 + 2 * (u % 2) + h, 0:n],
                                                qs[0:ROW_MAX, head, t * P:(t + 1) * P], ks[0:ROW_MAX, head, 0:n],
                                                start=True, stop=True)
                    last.then_inc(mx_ps, 1)

            def turn_max(b):
                pe.wait_ge(msplit, 4 * (b + 1))
                for t in range(TT):
                    last = nc.tensor.transpose(ps_mt[:, t * P:(t + 1) * P], ms[:, t].rearrange("p r h -> p (r h)"),
                                               idb_sb[:])
                last.then_inc(mT_ps, 1)

            def steps(a, f, p):
                if a is not None:
                    attention(a, f)
                if p is not None:
                    project(p, a)
                if f is not None:
                    if a is None:
                        pe.wait_ge(w3_used, TT * f)
                    else:
                        pe.wait_ge(exp_done, 2 * STEPS * (a + 1))
                    if p is not None:
                        pe.wait_ge(v_sbs, p + 1)
                        pe.wait_ge(lat_sb, p + 1)
                    gated(f)
                if a is not None:
                    if p is not None:
                        pe.wait_ge(terms, 8 * (p + 1))
                    attn_out(a)
                if f is not None:
                    for m in range(KF):
                        hidden(f, m, h1_sb, hid_a, g1_done, g2_done, l2_ps)
                if a is not None:
                    turn_x2(a)
                    pe.wait_ge(x2T_sb, a + 1)
                for m in range(KF):
                    if f is not None:
                        hidden(f, m, h2_sb, hid_b, g2_done, g3_done, l3_ps)
                    if p is not None:
                        if m == 0 and a is None:
                            pe.wait_ge(terms, 8 * (p + 1))
                        max_scores(p, m)
                if p is not None:
                    turn_max(p)
                    pe.wait_ge(mT_sb, p + 1)
                if f is not None:
                    output(f)

            pe.wait_ge(sums_clear, 1)
            pe.wait_ge(weights_in, WEIGHT_LOADS * 16)
            pe.wait_ge(wffn_in, 160)
            schedule(pe, steps)


def tables():
    inv = 1.0 / 10000.0 ** (np.arange(0, D, 2, dtype=np.float32) / D)
    ang = np.outer(np.arange(T, dtype=np.float32), inv)
    cos, sin = (np.repeat(f(ang).astype(np.float32).T, H, axis=0) for f in (np.cos, np.sin))
    tile, page = np.arange(T) // P, np.arange(T) // PAGE % 2
    q, k = np.zeros((2, P - ROWS_QK, T), np.float32)
    for t in range(TT):
        q[t] = MASKED * ((tile == t) & (page == 0))
        k[t] = (tile == t) & (page == 1)
    k[TT:TT + 3] = 1.0
    return cos, sin, q, k


def kernel(L0_attn_x, L0_attn_wq, L0_attn_w_down, L0_attn_wk_up, L0_attn_wv_up, L0_attn_wo,
           L0_ffn_w1_w, L0_ffn_w1_s, L0_ffn_w2_w, L0_ffn_w2_s, L0_ffn_h1_w, L0_ffn_h1_s,
           L0_ffn_h2_w, L0_ffn_h2_s, L0_ffn_w3_w, L0_ffn_w3_s):
    import ml_dtypes
    import concourse.bacc as bacc
    from concourse.bass_utils import run_bass_kernel_spmd

    cols = np.arange(E).reshape(H, D // 2, 2).transpose(2, 1, 0).reshape(E)
    cos, sin, qconst, kconst = tables()
    per_tile = lambda s: np.asarray(s).reshape(KF, P).T
    data = dict(
        x=L0_attn_x, wq=np.asarray(L0_attn_wq)[:, cols], wd=L0_attn_w_down,
        wk=np.asarray(L0_attn_wk_up)[:, cols], wv=L0_attn_wv_up, wo=L0_attn_wo,
        w1=np.asarray(L0_ffn_w1_w).T, s1=per_tile(L0_ffn_w1_s), w2=np.asarray(L0_ffn_w2_w).T,
        s2=per_tile(L0_ffn_w2_s), h1=np.asarray(L0_ffn_h1_w).T, sh1=per_tile(L0_ffn_h1_s),
        h2=np.asarray(L0_ffn_h2_w).T, sh2=per_tile(L0_ffn_h2_s), w3=np.asarray(L0_ffn_w3_w).T,
        s3=np.asarray(L0_ffn_w3_s).reshape(1, E), cos=cos, sin=sin,
        qconst=qconst.astype(ml_dtypes.bfloat16), kconst=kconst.astype(ml_dtypes.bfloat16),
        ident=np.eye(P, dtype=np.float32), identb=np.eye(P, dtype=ml_dtypes.bfloat16))
    nc = bacc.Bacc("TRN2", target_bir_lowering=False, num_devices=1)
    arrays = {f"in_{n}": np.ascontiguousarray(a) for n, a in data.items()}
    args = [nc.dram_tensor(n, a.shape, mybir.dt.from_np(a.dtype), kind="ExternalInput").ap()
            for n, a in arrays.items()]
    args.append(nc.dram_tensor("out", (B, T, E), F32, kind="ExternalOutput").ap())
    program(nc, *args)
    return run_bass_kernel_spmd(nc, [arrays], core_ids=[0]).results[0]["out"]
```

```python
from contextlib import ExitStack

import numpy as np

import concourse.bass as bass
from concourse import mybir

F32 = mybir.dt.float32
BF16 = mybir.dt.bfloat16
F16 = mybir.dt.float16
I32 = mybir.dt.int32
ALU = mybir.AluOpType
ACT = mybir.ActivationFunctionType
AX = mybir.AxisListType

P = 128
B, T, E = 16, 512, 256
L = E // 2
H, D = 16, 16
F = 1024
PAGE = 64
TT = T // P
KE = E // P
KF = F // P
HG = 4
NG = H // HG
VW = D + 1
COL = 32
LOW = 2048.0
S_IN, S_HID = 1.0 / 16, 1.0 / 32
OUT_SCALE = 0.125
SLOTS = 3
EPS = 1e-5
SCALE = float(D) ** -0.5
MASKED = -1e30
ROWS_QK = 7 * D
ROW_MASK = ROWS_QK
ROW_MAX = ROW_MASK + TT
Q_STACK = ((0, 0, 1), (0, 1, 1), (0, 2, 1), (1, 3, 1), (1, 4, 1), (1, 5, 1), (2, 6, 1))
K_STACK = ((0, 0, 3), (0, 3, 3), (0, 6, 1))
STACKS = 16 * (len(Q_STACK) + len(K_STACK))
WEIGHT_LOADS = 11
LN = TT + 7
STEPS = NG * TT


def program(nc, x, wq, wd, wk, wv, wo, w1, s1, w2, s2, h1, sh1, h2, sh2, w3, s3,
            cos, sin, qconst, kconst, ident, identb, out):
    scratch = nc.dram_tensor("qk_parts", [2, 3, 2, P, T], BF16).ap()
    max_scratch = nc.dram_tensor("max_parts", [3 * H, T], BF16).ap()
    with ExitStack() as ctx:
        def sb(name, shape, dt=F32):
            return ctx.enter_context(nc.sbuf_tensor(name, shape, dt))

        def sem(name):
            return ctx.enter_context(nc.semaphore(name))

        w1_sb, w2_sb = sb("w1_sb", [P, KE, F]), sb("w2_sb", [P, KE, F])
        h1_sb, h2_sb = sb("h1_sb", [P, KF, F]), sb("h2_sb", [P, KF, F])
        w3_sb = sb("w3_sb", [P, KF, E])
        wq_sb, wo_sb = sb("wq_sb", [P, KE, E]), sb("wo_sb", [P, KE, E])
        wd_sb = sb("wd_sb", [P, KE, L])
        wk_sb, wv_sb = sb("wk_sb", [P, E]), sb("wv_sb", [P, E])
        cos_sb, sin_sb = sb("cos_sb", [P, T]), sb("sin_sb", [P, T])
        s_sb = sb("s_sb", [P, 4, KF])
        s3_sb = sb("s3_sb", [P, E])
        id_sb, idb_sb = sb("id_sb", [P, P]), sb("idb_sb", [P, P], BF16)
        half = sb("half", [P, TT])

        qs, ks = sb("qs", [P, H, T], BF16), sb("ks", [P, H, T], BF16)
        v_sb = sb("v_sb", [P, TT, H, VW])
        rot = sb("rot", [P, 2, 2, T])
        parts = sb("parts", [P, 2, 3, T], BF16)
        mx, mr = sb("mx", [P, TT, H]), sb("mr", [P, TT, H])
        ms = sb("ms", [P, TT, 8, H], BF16)
        rsum = sb("rsum", [P, TT, HG])
        on = sb("on", [P, TT, E])
        x1n, x1o = sb("x1n", [P, TT, E]), sb("x1o", [P, TT, E])
        turned = sb("turned", [P, KE, T])
        bad = sb("bad", [P, 32])
        bad_row = sb("bad_row", [P, 1])
        bad_all = sb("bad_all", [P, 1])
        flag = sb("flag", [1, 1], I32)
        s_sq = sb("s_sq", [P, 4, KF])
        hid_a, hid_b = sb("hid_a", [P, KF, T]), sb("hid_b", [P, KF, T])
        probs = hid_b[:, :, :].rearrange("p (s h) t -> p s h t", s=2)
        tmp = sb("tmp", [P, 2, T])
        xt = hid_a[:, 0:TT * E // T, :].rearrange("p a (b e) -> p (a b) e", e=E)
        og = rot[:, 1, 1, :]
        mt = parts[0:3 * H, 0, 0, :]
        xnT = rot[:, 0, :, :]
        latT = rot[:, 1, 0, :]
        stage = tmp[:, :, :].rearrange("p a (b e) -> p (a b) e", e=E)
        arriving = hid_a[:, 2:2 + 2 * SLOTS, :].rearrange("p (s a) t -> p s (a t)", s=SLOTS)
        chunks = [(w_sb, w, k, F, 1) for w_sb, w, n in ((w1_sb, w1, KE), (w2_sb, w2, KE), (h1_sb, h1, KF),
                                                        (h2_sb, h2, KF)) for k in range(n)]
        chunks += [(w3_sb, w3, k, E, F // E) for k in range(0, KF, F // E)]

        def f16(tile):
            n = tile.shape[1]
            two = tile.bitcast(F16)
            return two[:, 0:n], two[:, n:2 * n]

        st = [sb(f"st{n}", [P, TT, 6]) for n in range(4)]
        mv = [sb(f"mv{n}", [P, 3, TT]) for n in range(4)]
        rs = [sb(f"rs{n}", [P, TT]) for n in range(4)]

        ps = ctx.enter_context(nc.psum_tensor("ps", [P, 8, T], F32))
        ps_mt = ps[:, 4, :].bitcast(BF16)[:, 0:T]

        weights_in, wffn_in, const_in, pool_const = (sem(n) for n in
                                                     ("weights_in", "wffn_in", "const_in", "pool_const"))
        chunk_in = [sem(f"chunk_in{n}") for n in range(SLOTS)]
        converted, scales_seen, bad_summed, bad_total, flag_ready, float32_in = (
            sem(n) for n in ("converted", "scales_seen", "bad_summed", "bad_total", "flag_ready", "float32_in"))
        gated, split1, split2, split3, split_x, x2_done, gelu2_done, gelu3_done = (
            sem(n) for n in ("gated", "split1", "split2", "split3", "split_x", "x2_done", "gelu2_done", "gelu3_done"))
        sums_clear, max_out = sem("sums_clear"), sem("max_out")
        scratch_in = [sem(f"scratch_in{n}") for n in range(2)]
        x_in, xr_in, stack_in, mrow_in, out_done = (
            sem(n) for n in ("x_in", "xr_in", "stack_in", "mrow_in", "out_done"))
        stats = [sem(f"stats{n}") for n in range(4)]
        rstd = [sem(f"rstd{n}") for n in range(4)]
        xn_ready, x1_kept, x1_part, x1_ready, xn2_ready, y_done, out_ready = (
            sem(n) for n in ("xn_ready", "x1_kept", "x1_part", "x1_ready", "xn2_ready", "y_done", "out_ready"))
        xT_ps, lat_ps, qk_ps, v_ps, xT_sb, lat_sb, v_sbs = (
            sem(n) for n in ("xT_ps", "lat_ps", "qk_ps", "v_ps", "xT_sb", "lat_sb", "v_sbs"))
        terms, rotated, high_done, rest_done, mid_done, parts_ready = (
            sem(n) for n in ("terms", "rotated", "high_done", "rest_done", "mid_done", "parts_ready"))
        mx_ps, mx_used, msplit, mT_ps, mT_sb = (
            sem(n) for n in ("mx_ps", "mx_used", "msplit", "mT_ps", "mT_sb"))
        st_ps, exp_done, av_done, o_sb, o_ps, r_done, on_done = (
            sem(n) for n in ("st_ps", "exp_done", "av_done", "o_sb", "o_ps", "r_done", "on_done"))
        onT_ps, onT_sb, wo_ps, x2T_ps, x2T_sb = (
            sem(n) for n in ("onT_ps", "onT_sb", "wo_ps", "x2T_ps", "x2T_sb"))
        l1_ps, silu_done, g1_done, l2_ps, g2_done, l3_ps, g3_done, w3_ps, w3_used = (
            sem(n) for n in ("l1_ps", "silu_done", "g1_done", "l2_ps", "g2_done", "l3_ps", "g3_done",
                             "w3_ps", "w3_used"))

        def schedule(eng, steps, branch=False, before_general=None):
            def rest(fast):
                steps(1, 0, 2, fast)
                with eng.Fori(2, B - 1) as i:
                    steps(i, i - 1, i + 1, fast)
                steps(B - 1, B - 2, None, fast)
                steps(None, B - 1, None, fast)

            steps(None, None, 0, None)
            steps(0, None, 1, None)
            if not branch:
                rest(None)
                return
            eng.wait_ge(flag_ready, 1)
            found = eng.value_load(flag[0:1, 0:1])
            with eng.If(found < 1):
                rest(True)
            with eng.Else():
                if before_general:
                    before_general()
                rest(False)

        def later(b):
            return not (isinstance(b, int) and b == 0)

        block = ctx.enter_context(nc.Block())

        @block.sync
        def _(sp):
            def load_weights():
                for dst, src in ((wq_sb, wq), (wd_sb, wd), (wo_sb, wo)):
                    sp.dma_start(dst[:], src.rearrange("(k p) n -> p k n", p=P)).then_inc(weights_in, 16)
                for dst, src in ((wk_sb, wk), (wv_sb, wv), (cos_sb, cos), (sin_sb, sin)):
                    sp.dma_start(dst[:], src).then_inc(weights_in, 16)
                for dst, src in ((qs, qconst), (ks, kconst)):
                    sp.dma_start(dst[ROWS_QK:P, :, :],
                                 src.unsqueeze(1).to_broadcast([P - ROWS_QK, H, T])).then_inc(weights_in, 16)
                for dst, src in ((id_sb, ident), (idb_sb, identb)):
                    sp.dma_start(dst[:], src).then_inc(weights_in, 16)
                for n, s in enumerate((s1, s2, sh1, sh2)):
                    sp.dma_start(s_sb[:, n, :], s).then_inc(wffn_in, 16)
                sp.dma_start(s3_sb[:], s3.to_broadcast([P, E])).then_inc(wffn_in, 16)

            def load_chunks():
                for c, (_, src, k, n, m) in enumerate(chunks):
                    if c >= SLOTS:
                        sp.wait_ge(converted, 3 * (c - SLOTS + 1))
                    sp.dma_start(arriving[:, c % SLOTS, :].rearrange("p (k n) -> p k n", n=n),
                                 src.rearrange("(k p) n -> p k n", p=P)[:, k:k + m, :]
                                 ).then_inc(chunk_in[c % SLOTS], 16)

            def load_float32():
                for dst, src in ((w1_sb, w1), (w2_sb, w2), (h1_sb, h1), (h2_sb, h2), (w3_sb, w3)):
                    sp.dma_start(dst[:], src.rearrange("(k p) n -> p k n", p=P)).then_inc(float32_in, 16)

            def batch(dram, b):
                return dram[bass.ds(b, 1)].rearrange("a (t p) e -> p (a t) e", p=P)

            def load_x(b, f):
                if f is not None and later(f):
                    sp.wait_ge(w3_ps, TT * f)
                elif later(b):
                    sp.wait_ge(xT_ps, b)
                sp.dma_start(xt, batch(x, b)).then_inc(x_in, 16)

            def reload_x(b):
                if later(b):
                    sp.wait_ge(x1_kept, b)
                sp.dma_start(x1n[:], batch(x, b)).then_inc(xr_in, 16)

            def stacks(b):
                for n in range(4):
                    if n == 0 and later(b):
                        sp.wait_ge(stack_in, STACKS * b)
                    sp.wait_ge(parts_ready, 4 * b + n + 1)
                    sp.dma_start(scratch[n // 2, :, n % 2].rearrange("c p t -> p c t"),
                                 parts[:, n % 2]).then_inc(scratch_in[n % 2], 16)
                    if n % 2:
                        if n == 1 and later(b):
                            sp.wait_ge(av_done, STEPS * b)
                        for half_ in range(2):
                            sp.wait_ge(scratch_in[half_], 32 * b + 8 * (n + 1))
                        rows = scratch[n // 2].rearrange("c a (d h) t -> (c a d) (h t)", h=H)
                        for at, to, k in Q_STACK if n == 1 else K_STACK:
                            dst = (qs, ks)[n // 2][to * D:(to + k) * D].rearrange("p h t -> p (h t)")
                            sp.dma_start(dst, rows[at * D:(at + k) * D]).then_inc(stack_in, 16)

            def max_rows(b):
                sp.wait_ge(mT_sb, b + 1)
                sp.dma_start(max_scratch, mt).then_inc(max_out, 16)
                sp.wait_ge(max_out, 16 * (b + 1))
                sp.dma_start(qs[ROW_MAX:ROW_MAX + 3].rearrange("p h t -> p (h t)"),
                             max_scratch.rearrange("(r h) t -> r (h t)", h=H)).then_inc(mrow_in, 16)

            def store(b):
                sp.wait_ge(out_ready, b + 1)
                sp.dma_start(batch(out, b), stage).then_inc(out_done, 16)

            def steps(a, f, p, fast):
                if p is not None:
                    load_x(p, f)
                    if not later(p):
                        load_weights()
                if a is not None:
                    reload_x(a)
                    if not later(a):
                        load_chunks()
                if p is not None:
                    stacks(p)
                    max_rows(p)
                if f is not None:
                    store(f)

            schedule(sp, steps, True, load_float32)
            sp.wait_ge(out_done, 16 * B)

        @block.gpsimd
        def _(pool):
            def inverse_deviation(n, b):
                pool.wait_ge(stats[n], LN * (b + 1))
                nc.gpsimd.tensor_tensor(rs[n][:], mv[n][:, 2, :], half[:], ALU.pow).then_inc(rstd[n], 1)

            def split_rest(b, n):
                s = n % 2
                pool.wait_ge(high_done, 4 * b + n + 1)
                nc.gpsimd.tensor_tensor(rot[:, s, 1, :], rot[:, s, 0, :], parts[:, s, 0, :],
                                        ALU.subtract).then_inc(rest_done, 1)
                pool.wait_ge(rest_done, 4 * b + n + 1)
                pool.wait_ge(mid_done, 4 * b + n + 1)
                nc.gpsimd.tensor_tensor(parts[:, s, 2, :], rot[:, s, 1, :], parts[:, s, 1, :],
                                        ALU.subtract).then_inc(parts_ready, 1)

            def steps(a, f, p, fast):
                if p is not None:
                    inverse_deviation(0, p)
                if a is not None and not later(a):
                    pool.wait_ge(bad_summed, 1)
                    nc.gpsimd.partition_all_reduce(bad_all[:], bad_row[:], P, bass.bass_isa.ReduceOp.add
                                                   ).then_inc(bad_total, 1)
                if p is not None:
                    for n in range(4):
                        split_rest(p, n)
                if a is not None:
                    inverse_deviation(1, a)
                    inverse_deviation(2, a)
                if f is not None:
                    inverse_deviation(3, f)

            nc.gpsimd.memset(half[:], -0.5).then_inc(pool_const, 1)
            nc.gpsimd.memset(v_sb[:], 1.0).then_inc(pool_const, 1)
            pool.wait_ge(pool_const, 1)
            schedule(pool, steps)

        @block.scalar
        def _(act):
            def evac_xT(b):
                act.wait_ge(xT_ps, b + 1)
                if later(b):
                    act.wait_ge(parts_ready, 4 * b)
                nc.scalar.copy(xnT, ps[:, 6:8, :]).then_inc(xT_sb, 1)

            def evac_lat(b):
                act.wait_ge(lat_ps, b + 1)
                nc.scalar.copy(latT, ps[:, 2, :]).then_inc(lat_sb, 1)

            def evac_v(b):
                act.wait_ge(v_ps, b + 1)
                if not later(b):
                    act.wait_ge(pool_const, 2)
                nc.scalar.copy(v_sb[:, :, :, 0:D],
                               ps[:, 0:2, :].rearrange("p a (b h d) -> p (a b) h d", b=2, d=D)).then_inc(v_sbs, 1)

            def split_high(b, n):
                s = n % 2
                act.wait_ge(rotated, 4 * b + n + 1)
                if n >= 2 or later(b):
                    act.wait_ge(scratch_in[s], 32 * b + 16 * (n // 2))
                nc.scalar.copy(parts[:, s, 0, :], rot[:, s, 0, :]).then_inc(high_done, 1)
                act.wait_ge(rest_done, 4 * b + n + 1)
                nc.scalar.copy(parts[:, s, 1, :], rot[:, s, 1, :]).then_inc(mid_done, 1)

            def keep_x1(b):
                act.wait_ge(x1_ready, b + 1)
                if later(b):
                    act.wait_ge(out_ready, b)
                nc.scalar.copy(x1o[:], x1n[:]).then_inc(x1_kept, 1)

            def exps(b):
                for u in range(2 * STEPS):
                    g, k = u // 2, u // 2 % TT
                    n = T - P * k
                    act.wait_ge(st_ps, 2 * STEPS * b + u + 1)
                    if g >= 2:
                        act.wait_ge(av_done, STEPS * b + g - 1)
                    elif later(b):
                        act.wait_ge(av_done, STEPS * b + g - 1)
                    two = slice(2 * (u % 2), 2 * (u % 2) + 2)
                    nc.scalar.activation(probs[:, g % 2, two, 0:n], ps[:, two, 0:n], ACT.Exp,
                                         scale=SCALE).then_inc(exp_done, 1)

            def evac_onT(b):
                act.wait_ge(onT_ps, b + 1)
                nc.scalar.copy(turned[:], ps[:, 4:6, :]).then_inc(onT_sb, 1)

            def evac_x2T(b, f):
                act.wait_ge(x2T_ps, b + 1)
                if f is not None:
                    act.wait_ge(g2_done, 8 * (f + 1))
                nc.scalar.copy(tmp[:], ps[:, 4:6, :]).then_inc(x2T_sb, 1)

            def evac_mT(b):
                act.wait_ge(mT_ps, b + 1)
                if later(b):
                    act.wait_ge(mrow_in, 16 * b)
                nc.scalar.copy(mt, ps_mt[0:3 * H]).then_inc(mT_sb, 1)

            def silu(b, m):
                act.wait_ge(l1_ps, 8 * b + m + 1)
                if m < 2 and later(b):
                    act.wait_ge(out_done, 16 * b)
                elif m >= 2:
                    act.wait_ge(g1_done, 8 * b + m - 1)
                else:
                    act.wait_ge(x2_done, 1)
                nc.scalar.activation(tmp[:, m % 2, :], ps[:, 2 * (m % 2), :], ACT.Silu,
                                     scale=s_sb[:, 0, m:m + 1]).then_inc(silu_done, 1)

            def gelu(b, m, ready, n, done, used, before):
                act.wait_ge(ready, 8 * b + m + 1)
                if m >= 2:
                    act.wait_ge(used, 8 * b + m - 1)
                else:
                    act.wait_ge(*before)
                nc.scalar.activation(tmp[:, m % 2, :], ps[:, m % 4, :], ACT.Gelu,
                                     scale=s_sb[:, n, m:m + 1]).then_inc(done, 1)

            def steps(a, f, p, fast):
                if f is not None:
                    keep_x1(f)
                if a is not None:
                    exps(a)
                if p is not None:
                    evac_xT(p)
                    evac_lat(p)
                    evac_v(p)
                for m in range(KF):
                    if f is not None:
                        silu(f, m)
                    if p is not None and m % 2 == 1:
                        split_high(p, m // 2)
                if a is not None:
                    evac_onT(a)
                if f is not None:
                    for m in range(KF):
                        gelu(f, m, l2_ps, 2, gelu2_done, g2_done, (g1_done, 8 * (f + 1)))
                if a is not None:
                    evac_x2T(a, f)
                if f is not None:
                    for m in range(KF):
                        gelu(f, m, l3_ps, 3, gelu3_done, g3_done,
                             (g2_done, 8 * (f + 1)) if a is None else (x2_done, a + 1))
                if p is not None:
                    evac_mT(p)

            act.wait_ge(wffn_in, 80)
            schedule(act, steps)

        @block.vector
        def _(dve):
            def mean_variance(n, b, tiles):
                for t in range(TT):
                    nc.vector.bn_stats(st[n][:, t, :], tiles(t)).then_inc(stats[n], 1)
                mean, square = st[n][:, :, 1::3], st[n][:, :, 2::3]
                dve.wait_ge(stats[n], LN * b + TT)
                nc.vector.tensor_tensor(mv[n][:, 0, :], mean[:, :, 0], mean[:, :, 1], ALU.add).then_inc(stats[n], 1)
                nc.vector.tensor_tensor(mv[n][:, 1, :], mean[:, :, 0], mean[:, :, 1], ALU.subtract).then_inc(stats[n], 1)
                nc.vector.tensor_tensor(mv[n][:, 2, :], square[:, :, 0], square[:, :, 1], ALU.add).then_inc(stats[n], 1)
                dve.wait_ge(stats[n], LN * b + TT + 3)
                nc.vector.tensor_scalar(mv[n][:, 0, :], mv[n][:, 0, :], 0.5, None, ALU.mult).then_inc(stats[n], 1)
                nc.vector.tensor_scalar(mv[n][:, 2, :], mv[n][:, 2, :], 1.0 / E, EPS, ALU.mult,
                                        ALU.add).then_inc(stats[n], 1)
                nc.vector.scalar_tensor_tensor(out=mv[n][:, 1, :], in0=mv[n][:, 1, :], scalar=0.25,
                                               in1=mv[n][:, 1, :], op0=ALU.mult, op1=ALU.mult).then_inc(stats[n], 1)
                dve.wait_ge(stats[n], LN * b + TT + 6)
                nc.vector.tensor_tensor(mv[n][:, 2, :], mv[n][:, 2, :], mv[n][:, 1, :], ALU.add).then_inc(stats[n], 1)

            def normalise(n, b, dst, tiles, done):
                dve.wait_ge(rstd[n], b + 1)
                for t in range(TT):
                    nc.vector.tensor_scalar(dst(t), tiles(t), mv[n][:, 0, t:t + 1], rs[n][:, t:t + 1],
                                            ALU.subtract, ALU.mult).then_inc(done, 1)

            def norm_x(b):
                dve.wait_ge(x_in, 16 * b + 16)
                mean_variance(0, b, lambda t: xt[:, t, :])
                normalise(0, b, lambda t: xt[:, t, :], lambda t: xt[:, t, :], xn_ready)

            def heads_out(b):
                for g in range(NG):
                    if not later(b):
                        for c in range(g * len(chunks) // NG, (g + 1) * len(chunks) // NG):
                            convert(c)
                    dve.wait_ge(av_done, STEPS * b + TT * (g + 1))
                    if g or later(b):
                        dve.wait_ge(o_ps, NG * b + g)
                    nc.vector.tensor_copy(og, ps[:, 4, :]).then_inc(o_sb, 1)
                    dve.wait_ge(o_ps, NG * b + g + 1)
                    if g or later(b):
                        dve.wait_ge(on_done, NG * b + g)
                    heads = ps[:, 5, :].rearrange("p (t h c) -> p t h c", t=TT, c=COL)
                    nc.vector.reciprocal(rsum[:], heads[:, :, :, D]).then_inc(r_done, 1)
                    dve.wait_ge(r_done, NG * b + g + 1)
                    if g == 0 and later(b):
                        dve.wait_ge(x2T_ps, b)
                    nc.vector.tensor_tensor(
                        on[:, :, g * HG * D:(g + 1) * HG * D].rearrange("p t (h d) -> p t h d", d=D),
                        heads[:, :, :, 0:D], rsum[:].unsqueeze(3).to_broadcast([P, TT, HG, D]),
                        ALU.mult).then_inc(on_done, 1)

            def rotate(b, n):
                s, bank = n % 2, 4 + 2 * (n // 2)
                dve.wait_ge(qk_ps, 2 * b + n // 2 + 1)
                if n == 0:
                    dve.wait_ge(v_ps, b + 1)
                if n >= 2:
                    dve.wait_ge(parts_ready, 4 * b + n - 1)
                first, second = ((cos_sb, sin_sb), (sin_sb, cos_sb))[n % 2]
                nc.vector.tensor_tensor(rot[:, s, 0, :], ps[:, bank, :], first[:], ALU.mult).then_inc(terms, 1)
                nc.vector.tensor_tensor(rot[:, s, 1, :], ps[:, bank + 1, :], second[:], ALU.mult).then_inc(terms, 1)
                dve.wait_ge(terms, 8 * b + 2 * n + 2)
                nc.vector.tensor_tensor(rot[:, s, 0, :], rot[:, s, 0, :], rot[:, s, 1, :],
                                        (ALU.subtract, ALU.add)[n % 2]).then_inc(rotated, 1)

            def split(src, high, low, scale, steps_done, at, done):
                nc.vector.tensor_scalar(high, src, scale, None, ALU.mult).then_inc(steps_done, 1)
                dve.wait_ge(steps_done, at + 1)
                nc.vector.scalar_tensor_tensor(out=src, in0=src, scalar=scale, in1=high, op0=ALU.mult,
                                               op1=ALU.subtract).then_inc(steps_done, 1)
                dve.wait_ge(steps_done, at + 2)
                nc.vector.tensor_scalar(low, src, LOW, None, ALU.mult).then_inc(done, 1)

            def gate(b, m, fast):
                dve.wait_ge(silu_done, 8 * b + m + 1)
                dst = tmp[:, m % 2, :]
                nc.vector.scalar_tensor_tensor(out=dst, in0=ps[:, 2 * (m % 2) + 1, :],
                                               scalar=s_sb[:, 1, m:m + 1], in1=tmp[:, m % 2, :],
                                               op0=ALU.mult, op1=ALU.mult).then_inc(gated, 1)
                dve.wait_ge(gated, 8 * b + m + 1)
                if fast:
                    split(dst, *f16(hid_a[:, m, :]), 1.0, split1, 16 * b + 2 * m, g1_done)
                else:
                    nc.vector.tensor_copy(hid_a[:, m, :], dst).then_inc(g1_done, 1)

            def take(b, m, fast, ready, dst, scale, steps_done, done):
                dve.wait_ge(ready, 8 * b + m + 1)
                if fast:
                    split(tmp[:, m % 2, :], *f16(dst[:, m, :]), scale, steps_done, 16 * b + 2 * m, done)
                else:
                    nc.vector.tensor_copy(dst[:, m, :], tmp[:, m % 2, :]).then_inc(done, 1)

            def take_x2(b, fast):
                dve.wait_ge(x2T_sb, b + 1)
                if fast:
                    both = turned[:].bitcast(F16)
                    split(tmp[:], both[:, :, 0:T], both[:, :, T:2 * T], 1.0, split_x, 2 * b, x2_done)
                else:
                    nc.vector.tensor_copy(turned[:], tmp[:]).then_inc(x2_done, 1)

            def convert(c):
                w_sb, _, k, n, m = chunks[c]
                dve.wait_ge(chunk_in[c % SLOTS], 16 * (c // SLOTS + 1))
                w = arriving[:, c % SLOTS, :].rearrange("p (k n) -> p k n", n=n)
                both = w_sb[:, k:k + m, :].bitcast(F16)
                whole, low = both[:, :, 0:n], both[:, :, n:2 * n]
                nc.vector.tensor_scalar(low, w, 1.0 / LOW, 1.0 / LOW, ALU.mult, ALU.min).then_inc(converted, 1)
                dve.wait_ge(converted, 3 * c + 1)
                nc.vector.tensor_scalar(whole, low, -1.0 / LOW, LOW, ALU.max, ALU.mult).then_inc(converted, 1)
                dve.wait_ge(converted, 3 * c + 2)
                nc.vector.scalar_tensor_tensor(out=w, in0=whole, scalar=1.0, in1=w, op0=ALU.mult,
                                               op1=ALU.not_equal, accum_out=bad[:, c:c + 1]).then_inc(converted, 1)

            def check_scales():
                nc.vector.tensor_tensor(s_sq[:], s_sb[:], s_sb[:], ALU.mult).then_inc(scales_seen, 1)
                dve.wait_ge(scales_seen, 1)
                for n, most in ((0, S_IN), (2, S_HID)):
                    nc.vector.tensor_scalar(s_sq[:, n:n + 2, :], s_sq[:, n:n + 2, :], most * most, None,
                                            ALU.is_gt).then_inc(scales_seen, 1)
                dve.wait_ge(scales_seen, 3)
                nc.vector.tensor_reduce(bad[:, len(chunks):len(chunks) + 1],
                                        s_sq[:].rearrange("p a k -> p (a k)"), AX.X, ALU.add).then_inc(scales_seen, 1)
                dve.wait_ge(scales_seen, 4)
                dve.wait_ge(converted, 3 * len(chunks))
                nc.vector.tensor_reduce(bad_row[:], bad[:, 0:len(chunks) + 1], AX.X, ALU.add).then_inc(bad_summed, 1)
                dve.wait_ge(bad_total, 1)
                nc.vector.tensor_copy(flag[:], bad_all[0:1, :]).then_inc(flag_ready, 1)

            def attn_norms(b):
                dve.wait_ge(wo_ps, b + 1)
                proj = lambda t: ps[:, 6 + t // 2, (t % 2) * E:(t % 2 + 1) * E]
                mean_variance(1, b, proj)
                normalise(1, b, lambda t: on[:, t, :], proj, x1_part)
                dve.wait_ge(x1_part, TT * (b + 1))
                dve.wait_ge(xr_in, 16 * (b + 1))
                nc.vector.tensor_tensor(x1n[:], x1n[:], on[:], ALU.add).then_inc(x1_ready, 1)
                dve.wait_ge(x1_ready, b + 1)
                mean_variance(2, b, lambda t: x1n[:, t, :])
                normalise(2, b, lambda t: on[:, t, :], lambda t: x1n[:, t, :], xn2_ready)

            def head_max(b, h2, t):
                u = TT * h2 + t
                n = P * (t + 1)
                dve.wait_ge(mx_ps, 32 * b + u + 1)
                two = slice(4 + 2 * (u % 2), 6 + 2 * (u % 2))
                nc.vector.tensor_reduce(mx[:, t, 2 * h2:2 * h2 + 2], ps[:, two, 0:n], AX.X,
                                        ALU.max).then_inc(mx_used, 1)

            def split_max(b):
                dve.wait_ge(mx_used, 32 * (b + 1))
                nc.vector.tensor_scalar(ms[:, :, 0, :], mx[:], -1.0, None, ALU.mult).then_inc(msplit, 1)
                dve.wait_ge(msplit, 4 * b + 1)
                nc.vector.scalar_tensor_tensor(out=mr[:], in0=mx[:], scalar=-1.0, in1=ms[:, :, 0, :],
                                               op0=ALU.mult, op1=ALU.subtract).then_inc(msplit, 1)
                dve.wait_ge(msplit, 4 * b + 2)
                nc.vector.tensor_copy(ms[:, :, 1, :], mr[:]).then_inc(msplit, 1)
                dve.wait_ge(msplit, 4 * b + 3)
                nc.vector.tensor_tensor(ms[:, :, 2, :], mr[:], ms[:, :, 1, :], ALU.subtract).then_inc(msplit, 1)

            def ffn_norm(b, fast):
                for t in range(TT):
                    dve.wait_ge(w3_ps, TT * b + t + 1)
                    nc.vector.scalar_tensor_tensor(out=stage[:, t, :], in0=ps[:, t, 0:E],
                                                   scalar=1.0 / OUT_SCALE if fast else 1.0, in1=s3_sb[:],
                                                   op0=ALU.mult, op1=ALU.mult).then_inc(w3_used, 1)
                dve.wait_ge(w3_used, TT * (b + 1))
                mean_variance(3, b, lambda t: stage[:, t, :])
                normalise(3, b, lambda t: stage[:, t, :], lambda t: stage[:, t, :], y_done)
                dve.wait_ge(y_done, TT * (b + 1))
                dve.wait_ge(x1_kept, b + 1)
                nc.vector.tensor_tensor(stage, stage, x1o[:], ALU.add).then_inc(out_ready, 1)

            def steps(a, f, p, fast):
                if f is not None and not later(f):
                    take_x2(f, fast)
                if p is not None:
                    norm_x(p)
                if a is not None:
                    heads_out(a)
                    if not later(a):
                        check_scales()
                for m in range(KF):
                    if f is not None:
                        gate(f, m, fast)
                    if p is not None and m % 2 == 1:
                        rotate(p, m // 2)
                if a is not None:
                    attn_norms(a)
                if f is not None:
                    for m in range(KF):
                        take(f, m, fast, gelu2_done, hid_b, 1.0, split2, g2_done)
                if a is not None and later(a):
                    take_x2(a, fast)
                for m in range(KF):
                    if p is not None:
                        for t in range(TT):
                            head_max(p, m, t)
                    if f is not None:
                        take(f, m, fast, gelu3_done, hid_a, OUT_SCALE if fast else 1.0, split3, g3_done)
                if p is not None:
                    split_max(p)
                if f is not None:
                    ffn_norm(f, fast)

            nc.vector.memset(ps[:, 4, :], 0.0).then_inc(sums_clear, 1)
            nc.vector.memset(ms[:], 0.0).then_inc(sums_clear, 1)
            dve.wait_ge(sums_clear, 2)
            dve.wait_ge(weights_in, WEIGHT_LOADS * 16)
            dve.wait_ge(wffn_in, 80)
            schedule(dve, steps, True)

        @block.tensor
        def _(pe):
            def transposes(src, bank):
                for k in range(KE):
                    for t in range(TT):
                        last = nc.tensor.transpose(ps[:, bank + k, t * P:(t + 1) * P],
                                                   src[:, t, k * P:(k + 1) * P], id_sb[:])
                return last

            def project(b, a):
                pe.wait_ge(xn_ready, TT * (b + 1))
                transposes(xt, 6).then_inc(xT_ps, 1)
                pe.wait_ge(xT_sb, b + 1)
                for k in range(KE):
                    last = nc.tensor.matmul(ps[:, 2, :], wd_sb[:, k, :], xnT[:, k, :], start=(k == 0), stop=(k == KE - 1))
                last.then_inc(lat_ps, 1)
                if a is not None:
                    pe.wait_ge(on_done, NG * (a + 1))
                for half_ in range(2):
                    for k in range(KE):
                        last = nc.tensor.matmul(ps[:, 4 + half_, :], wq_sb[:, k, half_ * P:(half_ + 1) * P], xnT[:, k, :],
                                                start=(k == 0), stop=(k == KE - 1))
                last.then_inc(qk_ps, 1)
                pe.wait_ge(lat_sb, b + 1)
                for half_ in range(2):
                    last = nc.tensor.matmul(ps[:, 6 + half_, :], wk_sb[:, half_ * P:(half_ + 1) * P], latT,
                                            start=True, stop=True)
                last.then_inc(qk_ps, 1)
                for t in range(TT):
                    last = nc.tensor.matmul(ps[:, t // 2, (t % 2) * E:(t % 2 + 1) * E], latT[:, t * P:(t + 1) * P],
                                            wv_sb[:], start=True, stop=True)
                last.then_inc(v_ps, 1)

            def scores(b, gk):
                g, k = gk // TT, gk % TT
                n = T - P * k
                for two in range(2):
                    u = 2 * gk + two
                    if u >= 2 or later(b):
                        pe.wait_ge(exp_done, 2 * STEPS * b + u - 1)
                    for h in range(2):
                        head = g * HG + 2 * two + h
                        last = nc.tensor.matmul(ps[:, 2 * two + h, 0:n], ks[:, head, k * P:(k + 1) * P],
                                                qs[:, head, k * P:T], start=True, stop=True)
                    last.then_inc(st_ps, 1)

            def weigh(b, gk):
                g, k = gk // TT, gk % TT
                n = T - P * k
                pe.wait_ge(exp_done, 2 * (STEPS * b + gk + 1))
                if k == 0 and (g or later(b)):
                    pe.wait_ge(o_sb, NG * b + g)
                for h in range(HG):
                    last = nc.tensor.matmul(ps[h * COL:h * COL + VW, 4, k * P:T], v_sb[:, k, g * HG + h, :],
                                            probs[:, gk % 2, h, 0:n], start=(k == 0), stop=(k == TT - 1),
                                            skip_group_check=True)
                last.then_inc(av_done, 1)

            def turn_group(b, g):
                pe.wait_ge(o_sb, NG * b + g + 1)
                if g or later(b):
                    pe.wait_ge(on_done, NG * b + g)
                for t in range(TT):
                    last = nc.tensor.transpose(ps[:, 5, t * P:(t + 1) * P], og[:, t * P:(t + 1) * P], id_sb[:])
                last.then_inc(o_ps, 1)

            def attention(b, f_before):
                pe.wait_ge(stack_in, STACKS * (b + 1))
                pe.wait_ge(mrow_in, 16 * (b + 1))
                pe.wait_ge(v_sbs, b + 1)
                if f_before is not None and later(f_before):
                    pe.wait_ge(w3_used, TT * f_before)
                scores(b, 0)
                for gk in range(STEPS):
                    if gk + 1 < STEPS:
                        scores(b, gk + 1)
                    weigh(b, gk)
                    if gk % TT == 1 and gk > TT:
                        turn_group(b, gk // TT - 1)
                turn_group(b, NG - 1)

            def products(out_, w, cols, src, tokens, fast, weights_first=True):
                pairs = []
                for k in range(src.shape[1]):
                    if fast:
                        pairs += list(zip(f16(w[:, k, :]), f16(src[:, k, :])))
                    else:
                        pairs.append((w[:, k, :], src[:, k, :]))
                for n, (w_k, src_k) in enumerate(pairs):
                    lhs, rhs = (w_k[:, cols], src_k[:, tokens]) if weights_first else (src_k[:, tokens], w_k[:, cols])
                    last = nc.tensor.matmul(out_, lhs, rhs, start=(n == 0), stop=(n == len(pairs) - 1))
                return last

            def gated_in(b, fast):
                pe.wait_ge(x2_done, b + 1)
                for m in range(KF):
                    if m >= 2:
                        pe.wait_ge(gated, 8 * b + m - 1)
                    for w, bank in ((w1_sb, 0), (w2_sb, 1)):
                        last = products(ps[:, 2 * (m % 2) + bank, :], w, slice(m * P, (m + 1) * P),
                                        turned, slice(0, T), fast)
                    last.then_inc(l1_ps, 1)

            def hidden(b, m, w, src, ready, own, done, fast):
                pe.wait_ge(ready, 8 * (b + 1))
                if m >= 4:
                    pe.wait_ge(own, 8 * b + m - 3)
                products(ps[:, m % 4, :], w, slice(m * P, (m + 1) * P), src, slice(0, T), fast).then_inc(done, 1)

            def output(b, fast):
                pe.wait_ge(g3_done, 8 * (b + 1))
                for t in range(TT):
                    products(ps[:, t, 0:E], w3_sb, slice(0, E), hid_a, slice(t * P, (t + 1) * P), fast,
                             weights_first=False).then_inc(w3_ps, 1)

            def attn_out(b):
                pe.wait_ge(on_done, NG * (b + 1))
                transposes(on, 4).then_inc(onT_ps, 1)
                pe.wait_ge(onT_sb, b + 1)
                for t in range(TT):
                    for k in range(KE):
                        last = nc.tensor.matmul(ps[:, 6 + t // 2, (t % 2) * E:(t % 2 + 1) * E],
                                                turned[:, k, t * P:(t + 1) * P], wo_sb[:, k, :],
                                                start=(k == 0), stop=(k == KE - 1))
                last.then_inc(wo_ps, 1)

            def turn_x2(b):
                pe.wait_ge(xn2_ready, TT * (b + 1))
                transposes(on, 4).then_inc(x2T_ps, 1)

            def max_scores(b, h2):
                pe.wait_ge(stack_in, STACKS * (b + 1))
                for t in range(TT):
                    u = TT * h2 + t
                    n = P * (t + 1)
                    if u >= 2 or later(b):
                        pe.wait_ge(mx_used, 32 * b + u - 1)
                    for h in range(2):
                        head = 2 * h2 + h
                        last = nc.tensor.matmul(ps[:, 4 + 2 * (u % 2) + h, 0:n],
                                                qs[0:ROW_MAX, head, t * P:(t + 1) * P], ks[0:ROW_MAX, head, 0:n],
                                                start=True, stop=True)
                    last.then_inc(mx_ps, 1)

            def turn_max(b):
                pe.wait_ge(msplit, 4 * (b + 1))
                for t in range(TT):
                    last = nc.tensor.transpose(ps_mt[:, t * P:(t + 1) * P], ms[:, t].rearrange("p r h -> p (r h)"),
                                               idb_sb[:])
                last.then_inc(mT_ps, 1)

            def steps(a, f, p, fast):
                if a is not None:
                    attention(a, f)
                if p is not None:
                    project(p, a)
                if f is not None:
                    if a is None:
                        pe.wait_ge(w3_used, TT * f)
                    else:
                        pe.wait_ge(exp_done, 2 * STEPS * (a + 1))
                    if p is not None:
                        pe.wait_ge(v_sbs, p + 1)
                        pe.wait_ge(lat_sb, p + 1)
                    gated_in(f, fast)
                if a is not None:
                    if p is not None:
                        pe.wait_ge(terms, 8 * (p + 1))
                    attn_out(a)
                if f is not None:
                    for m in range(KF):
                        hidden(f, m, h1_sb, hid_a, g1_done, gelu2_done, l2_ps, fast)
                if a is not None:
                    turn_x2(a)
                    pe.wait_ge(x2T_sb, a + 1)
                for m in range(KF):
                    if f is not None:
                        hidden(f, m, h2_sb, hid_b, g2_done, gelu3_done, l3_ps, fast)
                    if p is not None:
                        if m == 0 and a is None:
                            pe.wait_ge(terms, 8 * (p + 1))
                        max_scores(p, m)
                if p is not None:
                    turn_max(p)
                    pe.wait_ge(mT_sb, p + 1)
                if f is not None:
                    output(f, fast)

            pe.wait_ge(sums_clear, 1)
            pe.wait_ge(weights_in, WEIGHT_LOADS * 16)
            schedule(pe, steps, True, lambda: pe.wait_ge(float32_in, 80))


def tables():
    inv = 1.0 / 10000.0 ** (np.arange(0, D, 2, dtype=np.float32) / D)
    ang = np.outer(np.arange(T, dtype=np.float32), inv)
    cos, sin = (np.repeat(f(ang).astype(np.float32).T, H, axis=0) for f in (np.cos, np.sin))
    tile, page = np.arange(T) // P, np.arange(T) // PAGE % 2
    q, k = np.zeros((2, P - ROWS_QK, T), np.float32)
    for t in range(TT):
        q[t] = MASKED * ((tile == t) & (page == 0))
        k[t] = (tile == t) & (page == 1)
    k[TT:TT + 3] = 1.0
    return cos, sin, q, k


def kernel(L0_attn_x, L0_attn_wq, L0_attn_w_down, L0_attn_wk_up, L0_attn_wv_up, L0_attn_wo,
           L0_ffn_w1_w, L0_ffn_w1_s, L0_ffn_w2_w, L0_ffn_w2_s, L0_ffn_h1_w, L0_ffn_h1_s,
           L0_ffn_h2_w, L0_ffn_h2_s, L0_ffn_w3_w, L0_ffn_w3_s):
    import ml_dtypes
    import concourse.bacc as bacc
    from concourse.bass_utils import run_bass_kernel_spmd

    cols = np.arange(E).reshape(H, D // 2, 2).transpose(2, 1, 0).reshape(E)
    cos, sin, qconst, kconst = tables()
    per_tile = lambda s: np.asarray(s).reshape(KF, P).T
    data = dict(
        x=L0_attn_x, wq=np.asarray(L0_attn_wq)[:, cols], wd=L0_attn_w_down,
        wk=np.asarray(L0_attn_wk_up)[:, cols], wv=L0_attn_wv_up, wo=L0_attn_wo,
        w1=np.asarray(L0_ffn_w1_w).T, s1=per_tile(L0_ffn_w1_s), w2=np.asarray(L0_ffn_w2_w).T,
        s2=per_tile(L0_ffn_w2_s), h1=np.asarray(L0_ffn_h1_w).T, sh1=per_tile(L0_ffn_h1_s),
        h2=np.asarray(L0_ffn_h2_w).T, sh2=per_tile(L0_ffn_h2_s), w3=np.asarray(L0_ffn_w3_w).T,
        s3=np.asarray(L0_ffn_w3_s).reshape(1, E), cos=cos, sin=sin,
        qconst=qconst.astype(ml_dtypes.bfloat16), kconst=kconst.astype(ml_dtypes.bfloat16),
        ident=np.eye(P, dtype=np.float32), identb=np.eye(P, dtype=ml_dtypes.bfloat16))
    nc = bacc.Bacc("TRN2", target_bir_lowering=False, num_devices=1)
    arrays = {f"in_{n}": np.ascontiguousarray(a) for n, a in data.items()}
    args = [nc.dram_tensor(n, a.shape, mybir.dt.from_np(a.dtype), kind="ExternalInput").ap()
            for n, a in arrays.items()]
    args.append(nc.dram_tensor("out", (B, T, E), F32, kind="ExternalOutput").ap())
    program(nc, *args)
    return run_bass_kernel_spmd(nc, [arrays], core_ids=[0]).results[0]["out"]
```

```python
from contextlib import ExitStack

import numpy as np

import concourse.bass as bass
from concourse import mybir

F32 = mybir.dt.float32
BF16 = mybir.dt.bfloat16
F16 = mybir.dt.float16
I32 = mybir.dt.int32
ALU = mybir.AluOpType
ACT = mybir.ActivationFunctionType
AX = mybir.AxisListType

P = 128
B, T, E = 16, 512, 256
L = E // 2
H, D = 16, 16
F = 1024
PAGE = 64
TT = T // P
KE = E // P
KF = F // P
HG = 4
NG = H // HG
VW = D + 1
COL = 32
LOW = 2048.0
S_IN, S_HID = 1.0 / 16, 1.0 / 32
OUT_SCALE = 0.125
SLOTS = 3
EPS = 1e-5
SCALE = float(D) ** -0.5
MASKED = -1e30
ROWS_QK = 7 * D
ROW_MASK = ROWS_QK
ROW_MAX = ROW_MASK + TT
Q_STACK = ((0, 0, 1), (0, 1, 1), (0, 2, 1), (1, 3, 1), (1, 4, 1), (1, 5, 1), (2, 6, 1))
K_STACK = ((0, 0, 3), (0, 3, 3), (0, 6, 1))
STACKS = 16 * (len(Q_STACK) + len(K_STACK))
WEIGHT_LOADS = 11
LN = TT + 7
OUT_ORDER = (3, 2, 0, 1)
L1_BANKS = (0, 2, 6)
STEPS = NG * TT


def program(nc, x, wq, wd, wk, wv, wo, w1, s1, w2, s2, h1, sh1, h2, sh2, w3, s3,
            cos, sin, qconst, kconst, ident, identb, out):
    scratch = nc.dram_tensor("qk_parts", [2, 3, 2, P, T], BF16).ap()
    max_scratch = nc.dram_tensor("max_parts", [2, 3 * H, T], BF16).ap()
    with ExitStack() as ctx:
        def sb(name, shape, dt=F32):
            return ctx.enter_context(nc.sbuf_tensor(name, shape, dt))

        def sem(name):
            return ctx.enter_context(nc.semaphore(name))

        w1_sb, w2_sb = sb("w1_sb", [P, KE, F]), sb("w2_sb", [P, KE, F])
        h1_sb, h2_sb = sb("h1_sb", [P, KF, F]), sb("h2_sb", [P, KF, F])
        w3_sb = sb("w3_sb", [P, KF, E])
        wq_sb, wo_sb = sb("wq_sb", [P, KE, E]), sb("wo_sb", [P, KE, E])
        wd_sb = sb("wd_sb", [P, KE, L])
        wk_sb, wv_sb = sb("wk_sb", [P, E]), sb("wv_sb", [P, E])
        cos_sb, sin_sb = sb("cos_sb", [P, T]), sb("sin_sb", [P, T])
        s_sb = sb("s_sb", [P, 4, KF])
        s3_sb = sb("s3_sb", [P, E])
        id_sb, idb_sb = sb("id_sb", [P, P]), sb("idb_sb", [P, P], BF16)
        half, zero = sb("half", [P, TT]), sb("zero", [P, 1])

        qs, ks = sb("qs", [P, H, T], BF16), sb("ks", [P, H, T], BF16)
        v_sb = sb("v_sb", [P, TT, H, VW])
        rot = sb("rot", [P, 2, 2, T])
        parts = sb("parts", [P, 2, 3, T], BF16)
        mx, mr = sb("mx", [P, TT, H]), sb("mr", [P, TT, H])
        ms = sb("ms", [P, TT, 8, H], BF16)
        rsum = sb("rsum", [P, TT, HG])
        on = sb("on", [P, TT, E])
        x1n, x1o = sb("x1n", [P, TT, E]), sb("x1o", [P, TT, E])
        turned = sb("turned", [P, KE, T])
        bad = sb("bad", [P, 32])
        bad_row = sb("bad_row", [P, 1])
        bad_all = sb("bad_all", [P, 1])
        flag = sb("flag", [1, 1], I32)
        s_sq = sb("s_sq", [P, 4, KF])
        hid_a, hid_b = sb("hid_a", [P, KF, T]), sb("hid_b", [P, KF, T])
        probs = hid_b[:, :, :].rearrange("p (s h) t -> p s h t", s=2)
        tmp = sb("tmp", [P, 2, T])
        xt = hid_a[:, 0:TT * E // T, :].rearrange("p a (b e) -> p (a b) e", e=E)
        og = rot[:, 1, 1, :]
        mt = parts[0:3 * H, 0, 0, :]
        gates = (tmp[:, 0, :], tmp[:, 1, :], og)
        xnT = rot[:, 0, :, :]
        latT = rot[:, 1, 0, :]
        stage = tmp[:, :, :].rearrange("p a (b e) -> p (a b) e", e=E)
        arriving = hid_a[:, 2:2 + 2 * SLOTS, :].rearrange("p (s a) t -> p s (a t)", s=SLOTS)
        chunks = [(w_sb, w, k, F, 1) for w_sb, w, n in ((w1_sb, w1, KE), (w2_sb, w2, KE), (h1_sb, h1, KF),
                                                        (h2_sb, h2, KF)) for k in range(n)]
        chunks += [(w3_sb, w3, k, E, F // E) for k in range(0, KF, F // E)]

        def f16(tile):
            n = tile.shape[1]
            two = tile.bitcast(F16)
            return two[:, 0:n], two[:, n:2 * n]

        st = [sb(f"st{n}", [P, TT, 6]) for n in range(4)]
        mv = [sb(f"mv{n}", [P, 3, TT]) for n in range(4)]
        rs = [sb(f"rs{n}", [P, TT]) for n in range(4)]

        ps = ctx.enter_context(nc.psum_tensor("ps", [P, 8, T], F32))
        ps_mt = [ps[:, bank, :].bitcast(BF16)[:, 0:T] for bank in (3, 4)]

        weights_in, wffn_in, const_in, pool_const = (sem(n) for n in
                                                     ("weights_in", "wffn_in", "const_in", "pool_const"))
        chunk_in = [sem(f"chunk_in{n}") for n in range(SLOTS)]
        converted, scales_seen, bad_summed, bad_total, flag_ready, float32_in = (
            sem(n) for n in ("converted", "scales_seen", "bad_summed", "bad_total", "flag_ready", "float32_in"))
        high1, high2, high3, high_x, left1, left2, left3, left_x = (
            sem(n) for n in ("high1", "high2", "high3", "high_x", "left1", "left2", "left3", "left_x"))
        gated, x2_done, gelu2_done, gelu3_done = (
            sem(n) for n in ("gated", "x2_done", "gelu2_done", "gelu3_done"))
        sums_clear, max_out = sem("sums_clear"), sem("max_out")
        scratch_in = [sem(f"scratch_in{n}") for n in range(2)]
        mrow_in = [sem(f"mrow_in{n}") for n in range(2)]
        x_in, xr_in, stack_in, out_done = (sem(n) for n in ("x_in", "xr_in", "stack_in", "out_done"))
        stats = [sem(f"stats{n}") for n in range(4)]
        rstd = [sem(f"rstd{n}") for n in range(4)]
        xn_ready, x1_kept, x1_part, x1_ready, xn2_ready, y_done, out_ready = (
            sem(n) for n in ("xn_ready", "x1_kept", "x1_part", "x1_ready", "xn2_ready", "y_done", "out_ready"))
        xT_ps, lat_ps, qk_ps, v_ps, xT_sb, lat_sb, v_sbs = (
            sem(n) for n in ("xT_ps", "lat_ps", "qk_ps", "v_ps", "xT_sb", "lat_sb", "v_sbs"))
        terms, rotated, part_steps = (sem(n) for n in ("terms", "rotated", "part_steps"))
        mx_ps, mx_used, msplit, mT_ps, mT_sb = (
            sem(n) for n in ("mx_ps", "mx_used", "msplit", "mT_ps", "mT_sb"))
        st_ps, exp_done, av_done, o_sb, o_ps, r_done, on_done = (
            sem(n) for n in ("st_ps", "exp_done", "av_done", "o_sb", "o_ps", "r_done", "on_done"))
        onT_ps, onT_sb, wo_ps, x2T_ps, x2T_sb = (
            sem(n) for n in ("onT_ps", "onT_sb", "wo_ps", "x2T_ps", "x2T_sb"))
        l1_ps, silu_done, g1_done, l2_ps, g2_done, l3_ps, g3_done, w3_ps, w3_used = (
            sem(n) for n in ("l1_ps", "silu_done", "g1_done", "l2_ps", "g2_done", "l3_ps", "g3_done",
                             "w3_ps", "w3_used"))

        def schedule(eng, steps, branch=False, before_general=None):
            def rest(fast):
                steps(1, 0, 2, fast)
                with eng.Fori(2, B - 1) as i:
                    steps(i, i - 1, i + 1, fast)
                steps(B - 1, B - 2, None, fast)
                steps(None, B - 1, None, fast)

            steps(None, None, 0, None)
            steps(0, None, 1, None)
            if not branch:
                rest(None)
                return
            eng.wait_ge(flag_ready, 1)
            found = eng.value_load(flag[0:1, 0:1])
            with eng.If(found < 1):
                rest(True)
            with eng.Else():
                if before_general:
                    before_general()
                rest(False)

        def later(b):
            return not (isinstance(b, int) and b == 0)

        block = ctx.enter_context(nc.Block())

        @block.sync
        def _(sp):
            def load_weights():
                for dst, src in ((wq_sb, wq), (wd_sb, wd), (wo_sb, wo)):
                    sp.dma_start(dst[:], src.rearrange("(k p) n -> p k n", p=P)).then_inc(weights_in, 16)
                for dst, src in ((wk_sb, wk), (wv_sb, wv), (cos_sb, cos), (sin_sb, sin)):
                    sp.dma_start(dst[:], src).then_inc(weights_in, 16)
                for dst, src in ((qs, qconst), (ks, kconst)):
                    sp.dma_start(dst[ROWS_QK:P, :, :],
                                 src.unsqueeze(1).to_broadcast([P - ROWS_QK, H, T])).then_inc(weights_in, 16)
                for dst, src in ((id_sb, ident), (idb_sb, identb)):
                    sp.dma_start(dst[:], src).then_inc(weights_in, 16)
                for n, s in enumerate((s1, s2, sh1, sh2)):
                    sp.dma_start(s_sb[:, n, :], s).then_inc(wffn_in, 16)
                sp.dma_start(s3_sb[:], s3.to_broadcast([P, E])).then_inc(wffn_in, 16)

            def load_chunks():
                for c, (_, src, k, n, m) in enumerate(chunks):
                    if c >= SLOTS:
                        sp.wait_ge(converted, 3 * (c - SLOTS + 1))
                    sp.dma_start(arriving[:, c % SLOTS, :].rearrange("p (k n) -> p k n", n=n),
                                 src.rearrange("(k p) n -> p k n", p=P)[:, k:k + m, :]
                                 ).then_inc(chunk_in[c % SLOTS], 16)

            def load_float32():
                for dst, src in ((w1_sb, w1), (w2_sb, w2), (h1_sb, h1), (h2_sb, h2), (w3_sb, w3)):
                    sp.dma_start(dst[:], src.rearrange("(k p) n -> p k n", p=P)).then_inc(float32_in, 16)

            def batch(dram, b):
                return dram[bass.ds(b, 1)].rearrange("a (t p) e -> p (a t) e", p=P)

            def load_x(b, f):
                if f is not None and later(f):
                    sp.wait_ge(w3_ps, TT * f)
                elif later(b):
                    sp.wait_ge(xT_ps, b)
                sp.dma_start(xt, batch(x, b)).then_inc(x_in, 16)

            def reload_x(b):
                if later(b):
                    sp.wait_ge(x1_kept, b)
                sp.dma_start(x1n[:], batch(x, b)).then_inc(xr_in, 16)

            def stacks(b):
                for n in range(4):
                    if n == 0 and later(b):
                        sp.wait_ge(stack_in, STACKS * b)
                    sp.wait_ge(part_steps, 4 * (4 * b + n + 1))
                    sp.dma_start(scratch[n // 2, :, n % 2].rearrange("c p t -> p c t"),
                                 parts[:, n % 2]).then_inc(scratch_in[n % 2], 16)
                    if n % 2:
                        if n == 1 and later(b):
                            sp.wait_ge(av_done, STEPS * b)
                        for half_ in range(2):
                            sp.wait_ge(scratch_in[half_], 32 * b + 8 * (n + 1))
                        rows = scratch[n // 2].rearrange("c a (d h) t -> (c a d) (h t)", h=H)
                        for at, to, k in K_STACK if n == 1 else Q_STACK:
                            dst = (ks, qs)[n // 2][to * D:(to + k) * D].rearrange("p h t -> p (h t)")
                            sp.dma_start(dst, rows[at * D:(at + k) * D]).then_inc(stack_in, 16)

            def max_rows(b, half_):
                sp.wait_ge(mT_sb, 2 * b + half_ + 1)
                sp.dma_start(max_scratch[half_], mt).then_inc(max_out, 16)
                sp.wait_ge(max_out, 16 * (2 * b + half_ + 1))
                heads = slice(half_ * H // 2, (half_ + 1) * H // 2)
                sp.dma_start(qs[ROW_MAX:ROW_MAX + 3, heads, :],
                             max_scratch[half_].rearrange("(r h) t -> r h t", h=H)[:, heads, :]
                             ).then_inc(mrow_in[half_], 16)

            def store(b):
                sp.wait_ge(out_ready, b + 1)
                sp.dma_start(batch(out, b), stage).then_inc(out_done, 16)

            def steps(a, f, p, fast):
                if p is not None:
                    load_x(p, f)
                    if not later(p):
                        load_weights()
                    if f is not None and later(f):
                        store(f - 1)
                elif a is not None:
                    store(f - 1)
                if a is not None:
                    reload_x(a)
                    if not later(a):
                        load_chunks()
                if p is not None:
                    stacks(p)
                    max_rows(p, 0)
                    max_rows(p, 1)
                if p is None and f is not None:
                    store(f)

            schedule(sp, steps, True, load_float32)
            sp.wait_ge(out_done, 16 * B)

        @block.gpsimd
        def _(pool):
            def inverse_deviation(n, b):
                pool.wait_ge(stats[n], LN * (b + 1))
                nc.gpsimd.tensor_tensor(rs[n][:], mv[n][:, 2, :], half[:], ALU.pow).then_inc(rstd[n], 1)

            def split_rotated(b, n):
                s, at = n % 2, 16 * b + 4 * n
                left, term = rot[:, s, 0, :], rot[:, s, 1, :]
                high, mid, low = (parts[:, s, c, :] for c in range(3))
                nothing = zero[:].to_broadcast([P, T])
                if n >= 2 or later(b):
                    pool.wait_ge(scratch_in[s], 32 * b + 16 * (n // 2))
                pool.wait_ge(rotated, 4 * b + n + 1)
                nc.gpsimd.tensor_tensor(high, left, nothing, ALU.add).then_inc(part_steps, 1)
                pool.wait_ge(part_steps, at + 1)
                nc.gpsimd.tensor_tensor(term, left, high, ALU.subtract).then_inc(part_steps, 1)
                pool.wait_ge(part_steps, at + 2)
                nc.gpsimd.tensor_tensor(mid, term, nothing, ALU.add).then_inc(part_steps, 1)
                pool.wait_ge(part_steps, at + 3)
                nc.gpsimd.tensor_tensor(low, term, mid, ALU.subtract).then_inc(part_steps, 1)

            def steps(a, f, p, fast):
                if p is not None:
                    inverse_deviation(0, p)
                if a is not None and not later(a):
                    pool.wait_ge(bad_summed, 1)
                    nc.gpsimd.partition_all_reduce(bad_all[:], bad_row[:], P, bass.bass_isa.ReduceOp.add
                                                   ).then_inc(bad_total, 1)
                if a is not None:
                    inverse_deviation(1, a)
                if p is not None:
                    split_rotated(p, 0)
                    split_rotated(p, 1)
                if a is not None:
                    inverse_deviation(2, a)
                if p is not None:
                    split_rotated(p, 2)
                    split_rotated(p, 3)
                if f is not None:
                    inverse_deviation(3, f)

            nc.gpsimd.memset(half[:], -0.5).then_inc(pool_const, 1)
            nc.gpsimd.memset(v_sb[:], 1.0).then_inc(pool_const, 1)
            nc.gpsimd.memset(zero[:], 0.0).then_inc(pool_const, 1)
            pool.wait_ge(pool_const, 3)
            schedule(pool, steps)

        @block.scalar
        def _(act):
            def evac_xT(b):
                act.wait_ge(xT_ps, b + 1)
                if later(b):
                    act.wait_ge(part_steps, 16 * b)
                nc.scalar.copy(xnT, ps[:, 6:8, :]).then_inc(xT_sb, 1)

            def evac_lat(b):
                act.wait_ge(lat_ps, b + 1)
                nc.scalar.copy(latT, ps[:, 6, :]).then_inc(lat_sb, 1)

            def evac_v(b):
                act.wait_ge(v_ps, b + 1)
                if not later(b):
                    act.wait_ge(pool_const, 3)
                nc.scalar.copy(v_sb[:, :, :, 0:D],
                               ps[:, 0:2, :].rearrange("p a (b h d) -> p (a b) h d", b=2, d=D)).then_inc(v_sbs, 1)

            def keep_x1(b):
                act.wait_ge(x1_ready, b + 1)
                if later(b):
                    act.wait_ge(out_ready, b)
                nc.scalar.copy(x1o[:], x1n[:]).then_inc(x1_kept, 1)

            def exps(b, f, p):
                for u in range(2 * STEPS):
                    if f is not None and u == 12:
                        keep_x1(f)
                    if p is not None and u == 22:
                        evac_xT(p)
                    if p is not None and u == 28:
                        evac_lat(p)
                    g, k = u // 2, u // 2 % TT
                    n = T - P * k
                    act.wait_ge(st_ps, 2 * STEPS * b + u + 1)
                    if g >= 2:
                        act.wait_ge(av_done, STEPS * b + g - 1)
                    elif later(b):
                        act.wait_ge(av_done, STEPS * b + g - 1)
                    two = slice(2 * (u % 2), 2 * (u % 2) + 2)
                    nc.scalar.activation(probs[:, g % 2, two, 0:n], ps[:, two, 0:n], ACT.Exp,
                                         scale=SCALE).then_inc(exp_done, 1)

            def evac_onT(b):
                act.wait_ge(onT_ps, b + 1)
                nc.scalar.copy(turned[:], ps[:, 4:6, :]).then_inc(onT_sb, 1)

            def evac_x2T(b, fast):
                act.wait_ge(x2T_ps, b + 1)
                if not later(b):
                    nc.scalar.copy(tmp[:], ps[:, 6:8, :]).then_inc(x2T_sb, 1)
                elif fast:
                    nc.scalar.copy(turned[:].bitcast(F16)[:, :, 0:T], ps[:, 6:8, :]).then_inc(high_x, 1)

            def evac_mT(b, half_):
                act.wait_ge(mT_ps, 2 * b + half_ + 1)
                if half_ or later(b):
                    act.wait_ge(max_out, 16 * (2 * b + half_))
                nc.scalar.copy(mt, ps_mt[half_][0:3 * H]).then_inc(mT_sb, 1)

            def high(b, m, ready, src, dst, scale, done):
                act.wait_ge(ready, 8 * b + m + 1)
                nc.scalar.mul(f16(dst[:, m, :])[0], src, scale).then_inc(done, 1)

            def silu(b, m):
                act.wait_ge(l1_ps, 8 * b + m + 1)
                if m < 2 and later(b):
                    act.wait_ge(out_done, 16 * b)
                elif m >= 3:
                    act.wait_ge(g1_done, 8 * b + m - 2)
                else:
                    act.wait_ge(x2_done, 1)
                nc.scalar.activation(gates[m % 3], ps[:, L1_BANKS[m % 3], :], ACT.Silu,
                                     scale=s_sb[:, 0, m:m + 1]).then_inc(silu_done, 1)

            def gelu(b, m, ready, n, done, used, before, banks=4):
                act.wait_ge(ready, 8 * b + m + 1)
                if m >= 2:
                    act.wait_ge(used, 8 * b + m - 1)
                else:
                    act.wait_ge(*before)
                nc.scalar.activation(tmp[:, m % 2, :], ps[:, m % banks, :], ACT.Gelu,
                                     scale=s_sb[:, n, m:m + 1]).then_inc(done, 1)

            def steps(a, f, p, fast):
                if a is not None:
                    exps(a, f, p)
                else:
                    if f is not None:
                        keep_x1(f)
                    if p is not None:
                        evac_xT(p)
                        evac_lat(p)
                if f is not None:
                    silu(f, 0)
                    for m in range(KF):
                        if m + 1 < KF:
                            silu(f, m + 1)
                        if fast:
                            high(f, m, gated, gates[m % 3], hid_a, 1.0, high1)
                if a is not None:
                    evac_onT(a)
                if p is not None:
                    evac_v(p)
                for m in range(KF):
                    if a is not None and m == KF - 2:
                        evac_x2T(a, fast)
                    if f is not None:
                        gelu(f, m, l2_ps, 2, gelu2_done, g2_done, (g1_done, 8 * (f + 1)))
                        if fast:
                            high(f, m, gelu2_done, tmp[:, m % 2, :], hid_b, 1.0, high2)
                for m in range(KF):
                    if p is not None and m % 4 == 3:
                        evac_mT(p, m // 4)
                    if f is not None:
                        gelu(f, m, l3_ps, 3, gelu3_done, g3_done, (g2_done, 8 * f + 7 + m), 3)
                        if fast:
                            high(f, m, gelu3_done, tmp[:, m % 2, :], hid_a, OUT_SCALE, high3)

            act.wait_ge(wffn_in, 80)
            schedule(act, steps, True)

        @block.vector
        def _(dve):
            def mean_variance(n, b, tiles):
                for t in range(TT):
                    nc.vector.bn_stats(st[n][:, t, :], tiles(t)).then_inc(stats[n], 1)
                mean, square = st[n][:, :, 1::3], st[n][:, :, 2::3]
                dve.wait_ge(stats[n], LN * b + TT)
                nc.vector.tensor_tensor(mv[n][:, 0, :], mean[:, :, 0], mean[:, :, 1], ALU.add).then_inc(stats[n], 1)
                nc.vector.tensor_tensor(mv[n][:, 1, :], mean[:, :, 0], mean[:, :, 1], ALU.subtract).then_inc(stats[n], 1)
                nc.vector.tensor_tensor(mv[n][:, 2, :], square[:, :, 0], square[:, :, 1], ALU.add).then_inc(stats[n], 1)
                dve.wait_ge(stats[n], LN * b + TT + 3)
                nc.vector.tensor_scalar(mv[n][:, 0, :], mv[n][:, 0, :], 0.5, None, ALU.mult).then_inc(stats[n], 1)
                nc.vector.tensor_scalar(mv[n][:, 2, :], mv[n][:, 2, :], 1.0 / E, EPS, ALU.mult,
                                        ALU.add).then_inc(stats[n], 1)
                nc.vector.scalar_tensor_tensor(out=mv[n][:, 1, :], in0=mv[n][:, 1, :], scalar=0.25,
                                               in1=mv[n][:, 1, :], op0=ALU.mult, op1=ALU.mult).then_inc(stats[n], 1)
                dve.wait_ge(stats[n], LN * b + TT + 6)
                nc.vector.tensor_tensor(mv[n][:, 2, :], mv[n][:, 2, :], mv[n][:, 1, :], ALU.add).then_inc(stats[n], 1)

            def normalise(n, b, dst, tiles, done):
                dve.wait_ge(rstd[n], b + 1)
                for t in range(TT):
                    nc.vector.tensor_scalar(dst(t), tiles(t), mv[n][:, 0, t:t + 1], rs[n][:, t:t + 1],
                                            ALU.subtract, ALU.mult).then_inc(done, 1)

            def norm_x(b):
                dve.wait_ge(x_in, 16 * b + 16)
                mean_variance(0, b, lambda t: xt[:, t, :])
                normalise(0, b, lambda t: xt[:, t, :], lambda t: xt[:, t, :], xn_ready)

            def heads_out(b, p):
                for g in range(NG):
                    if not later(b):
                        for c in range(g * len(chunks) // NG, (g + 1) * len(chunks) // NG):
                            convert(c)
                    dve.wait_ge(av_done, STEPS * b + TT * (g + 1))
                    if g or later(b):
                        dve.wait_ge(o_ps, NG * b + g)
                    nc.vector.tensor_copy(og, ps[:, 4, :]).then_inc(o_sb, 1)
                    if p is not None and g == 0:
                        norm_x(p)
                    dve.wait_ge(o_ps, NG * b + g + 1)
                    if g or later(b):
                        dve.wait_ge(on_done, NG * b + g)
                    heads = ps[:, 5, :].rearrange("p (t h c) -> p t h c", t=TT, c=COL)
                    nc.vector.reciprocal(rsum[:], heads[:, :, :, D]).then_inc(r_done, 1)
                    dve.wait_ge(r_done, NG * b + g + 1)
                    if g == 0 and later(b):
                        dve.wait_ge(x2T_ps, b)
                    nc.vector.tensor_tensor(
                        on[:, :, g * HG * D:(g + 1) * HG * D].rearrange("p t (h d) -> p t h d", d=D),
                        heads[:, :, :, 0:D], rsum[:].unsqueeze(3).to_broadcast([P, TT, HG, D]),
                        ALU.mult).then_inc(on_done, 1)

            def rotate(b, n):
                s, bank = n % 2, (2, 4)[n // 2]
                if n == 0:
                    dve.wait_ge(qk_ps, 2 * (b + 1))
                if n >= 2:
                    dve.wait_ge(part_steps, 4 * (4 * b + n - 1))
                first, second = ((cos_sb, sin_sb), (sin_sb, cos_sb))[n % 2]
                nc.vector.tensor_tensor(rot[:, s, 0, :], ps[:, bank, :], first[:], ALU.mult).then_inc(terms, 1)
                nc.vector.tensor_tensor(rot[:, s, 1, :], ps[:, bank + 1, :], second[:], ALU.mult).then_inc(terms, 1)
                dve.wait_ge(terms, 8 * b + 2 * n + 2)
                nc.vector.tensor_tensor(rot[:, s, 0, :], rot[:, s, 0, :], rot[:, s, 1, :],
                                        (ALU.subtract, ALU.add)[n % 2]).then_inc(rotated, 1)

            def low_part(src, high, low, scale, left, at, done):
                nc.vector.scalar_tensor_tensor(out=src, in0=src, scalar=scale, in1=high, op0=ALU.mult,
                                               op1=ALU.subtract).then_inc(left, 1)
                dve.wait_ge(left, at)
                nc.vector.tensor_scalar(low, src, LOW, None, ALU.mult).then_inc(done, 1)

            def gate(b, m):
                dve.wait_ge(silu_done, 8 * b + m + 1)
                nc.vector.scalar_tensor_tensor(out=gates[m % 3], in0=ps[:, L1_BANKS[m % 3] + 1, :],
                                               scalar=s_sb[:, 1, m:m + 1], in1=gates[m % 3],
                                               op0=ALU.mult, op1=ALU.mult).then_inc(gated, 1)

            def take(b, m, fast, ready, high_done, src, dst, scale, left, done):
                if fast:
                    dve.wait_ge(high_done, 8 * b + m + 1)
                    low_part(src, *f16(dst[:, m, :]), scale, left, 8 * b + m + 1, done)
                else:
                    dve.wait_ge(ready, 8 * b + m + 1)
                    nc.vector.tensor_copy(dst[:, m, :], src).then_inc(done, 1)

            def take_x2(b, fast):
                if not later(b):
                    dve.wait_ge(x2T_sb, 1)
                    src = tmp[:]
                else:
                    src = ps[:, 6:8, :]
                if fast:
                    both = turned[:].bitcast(F16)
                    if not later(b):
                        nc.vector.tensor_copy(both[:, :, 0:T], src).then_inc(high_x, 1)
                    dve.wait_ge(high_x, b + 1)
                    low_part(src, both[:, :, 0:T], both[:, :, T:2 * T], 1.0, left_x, b + 1, x2_done)
                else:
                    dve.wait_ge(x2T_ps, b + 1)
                    nc.vector.tensor_copy(turned[:], src).then_inc(x2_done, 1)

            def convert(c):
                w_sb, _, k, n, m = chunks[c]
                dve.wait_ge(chunk_in[c % SLOTS], 16 * (c // SLOTS + 1))
                w = arriving[:, c % SLOTS, :].rearrange("p (k n) -> p k n", n=n)
                both = w_sb[:, k:k + m, :].bitcast(F16)
                whole, low = both[:, :, 0:n], both[:, :, n:2 * n]
                nc.vector.tensor_scalar(low, w, 1.0 / LOW, 1.0 / LOW, ALU.mult, ALU.min).then_inc(converted, 1)
                dve.wait_ge(converted, 3 * c + 1)
                nc.vector.tensor_scalar(whole, low, -1.0 / LOW, LOW, ALU.max, ALU.mult).then_inc(converted, 1)
                dve.wait_ge(converted, 3 * c + 2)
                nc.vector.scalar_tensor_tensor(out=w, in0=whole, scalar=1.0, in1=w, op0=ALU.mult,
                                               op1=ALU.not_equal, accum_out=bad[:, c:c + 1]).then_inc(converted, 1)

            def check_scales():
                nc.vector.tensor_tensor(s_sq[:], s_sb[:], s_sb[:], ALU.mult).then_inc(scales_seen, 1)
                dve.wait_ge(scales_seen, 1)
                for n, most in ((0, S_IN), (2, S_HID)):
                    nc.vector.tensor_scalar(s_sq[:, n:n + 2, :], s_sq[:, n:n + 2, :], most * most, None,
                                            ALU.is_gt).then_inc(scales_seen, 1)
                dve.wait_ge(scales_seen, 3)
                nc.vector.tensor_reduce(bad[:, len(chunks):len(chunks) + 1],
                                        s_sq[:].rearrange("p a k -> p (a k)"), AX.X, ALU.add).then_inc(scales_seen, 1)
                dve.wait_ge(scales_seen, 4)
                dve.wait_ge(converted, 3 * len(chunks))
                nc.vector.tensor_reduce(bad_row[:], bad[:, 0:len(chunks) + 1], AX.X, ALU.add).then_inc(bad_summed, 1)
                dve.wait_ge(bad_total, 1)
                nc.vector.tensor_copy(flag[:], bad_all[0:1, :]).then_inc(flag_ready, 1)

            def proj(t):
                return ps[:, 6 + t // 2, (t % 2) * E:(t % 2 + 1) * E]

            def attn_stats(b):
                dve.wait_ge(wo_ps, b + 1)
                mean_variance(1, b, proj)

            def add_attn(b):
                normalise(1, b, lambda t: on[:, t, :], proj, x1_part)
                dve.wait_ge(x1_part, TT * (b + 1))
                dve.wait_ge(xr_in, 16 * (b + 1))
                nc.vector.tensor_tensor(x1n[:], x1n[:], on[:], ALU.add).then_inc(x1_ready, 1)
                dve.wait_ge(x1_ready, b + 1)
                mean_variance(2, b, lambda t: x1n[:, t, :])

            def norm_x1(b):
                normalise(2, b, lambda t: on[:, t, :], lambda t: x1n[:, t, :], xn2_ready)

            def head_max(b, h2, t):
                u = TT * h2 + t
                n = P * (t + 1)
                dve.wait_ge(mx_ps, 32 * b + u + 1)
                two = slice(4 + 2 * (u % 2), 6 + 2 * (u % 2))
                nc.vector.tensor_reduce(mx[:, t, 2 * h2:2 * h2 + 2], ps[:, two, 0:n], AX.X,
                                        ALU.max).then_inc(mx_used, 1)

            def split_max(b, half_):
                heads, at = slice(half_ * H // 2, (half_ + 1) * H // 2), 8 * b + 4 * half_
                most, left = mx[:, :, heads], mr[:, :, heads]
                high, mid, low = (ms[:, :, c, heads] for c in range(3))
                dve.wait_ge(mx_used, 32 * b + 16 * (half_ + 1))
                if half_ or later(b):
                    dve.wait_ge(mT_ps, 2 * b + half_)
                nc.vector.tensor_scalar(high, most, -1.0, None, ALU.mult).then_inc(msplit, 1)
                dve.wait_ge(msplit, at + 1)
                nc.vector.scalar_tensor_tensor(out=left, in0=most, scalar=-1.0, in1=high,
                                               op0=ALU.mult, op1=ALU.subtract).then_inc(msplit, 1)
                dve.wait_ge(msplit, at + 2)
                nc.vector.tensor_copy(mid, left).then_inc(msplit, 1)
                dve.wait_ge(msplit, at + 3)
                nc.vector.tensor_tensor(low, left, mid, ALU.subtract).then_inc(msplit, 1)

            def ffn_norm(b, fast):
                for n, t in enumerate(OUT_ORDER):
                    dve.wait_ge(w3_ps, TT * b + n + 1)
                    nc.vector.scalar_tensor_tensor(out=stage[:, t, :], in0=ps[:, t, 0:E],
                                                   scalar=1.0 / OUT_SCALE if fast else 1.0, in1=s3_sb[:],
                                                   op0=ALU.mult, op1=ALU.mult).then_inc(w3_used, 1)
                dve.wait_ge(w3_used, TT * (b + 1))
                mean_variance(3, b, lambda t: stage[:, t, :])
                normalise(3, b, lambda t: stage[:, t, :], lambda t: stage[:, t, :], y_done)
                dve.wait_ge(y_done, TT * (b + 1))
                dve.wait_ge(x1_kept, b + 1)
                nc.vector.tensor_tensor(stage, stage, x1o[:], ALU.add).then_inc(out_ready, 1)

            def steps(a, f, p, fast):
                if f is not None and not later(f):
                    take_x2(f, fast)
                if p is not None and a is None:
                    norm_x(p)
                if a is not None:
                    heads_out(a, p)
                    if not later(a):
                        check_scales()
                def taken(n, m):
                    if f is not None:
                        ready, high_done, dst, left, done = ((gated, high1, hid_a, left1, g1_done),
                                                             (gelu2_done, high2, hid_b, left2, g2_done),
                                                             (gelu3_done, high3, hid_a, left3, g3_done))[n]
                        take(f, m, fast, ready, high_done, tmp[:, m % 2, :] if n else gates[m % 3], dst, OUT_SCALE if fast and n == 2 else 1.0, left, done)

                if f is not None:
                    gate(f, 0)
                    for m in range(KF):
                        if m + 1 < KF:
                            gate(f, m + 1)
                        taken(0, m)
                if a is not None:
                    attn_stats(a)
                if p is not None:
                    rotate(p, 0)
                    rotate(p, 1)
                if a is not None:
                    add_attn(a)
                for m in range(KF):
                    taken(1, m)
                    if p is not None and m in (0, 2):
                        rotate(p, 2 + m // 2)
                    if a is not None and m == 1:
                        norm_x1(a)
                    if a is not None and later(a) and m == KF - 3:
                        take_x2(a, fast)
                if p is not None:
                    for t in range(TT):
                        head_max(p, 0, t)
                for m in range(KF):
                    if p is not None and m + 1 < KF:
                        head_max(p, m + 1, 0)
                        head_max(p, m + 1, 1)
                    if m:
                        taken(2, m - 1)
                    if p is not None and m + 1 < KF:
                        head_max(p, m + 1, 2)
                        head_max(p, m + 1, 3)
                        if m % 4 == 2:
                            split_max(p, m // 4)
                taken(2, KF - 1)
                if f is not None:
                    ffn_norm(f, fast)

            nc.vector.memset(ps[:, 4, :], 0.0).then_inc(sums_clear, 1)
            nc.vector.memset(ms[:], 0.0).then_inc(sums_clear, 1)
            dve.wait_ge(sums_clear, 2)
            dve.wait_ge(weights_in, WEIGHT_LOADS * 16)
            dve.wait_ge(wffn_in, 80)
            schedule(dve, steps, True)

        @block.tensor
        def _(pe):
            def transposes(src, bank):
                for k in range(KE):
                    for t in range(TT):
                        last = nc.tensor.transpose(ps[:, bank + k, t * P:(t + 1) * P],
                                                   src[:, t, k * P:(k + 1) * P], id_sb[:])
                return last

            def turn_x(b):
                pe.wait_ge(xn_ready, TT * (b + 1))
                transposes(xt, 6).then_inc(xT_ps, 1)

            def latents(b):
                pe.wait_ge(xT_sb, b + 1)
                for k in range(KE):
                    last = nc.tensor.matmul(ps[:, 6, :], wd_sb[:, k, :], xnT[:, k, :], start=(k == 0), stop=(k == KE - 1))
                last.then_inc(lat_ps, 1)

            def project_kv(b, f):
                if f is not None:
                    pe.wait_ge(gated, 8 * f + 7)
                pe.wait_ge(lat_sb, b + 1)
                for t in range(TT):
                    last = nc.tensor.matmul(ps[:, t // 2, (t % 2) * E:(t % 2 + 1) * E], latT[:, t * P:(t + 1) * P],
                                            wv_sb[:], start=True, stop=True)
                last.then_inc(v_ps, 1)
                if f is not None:
                    pe.wait_ge(gated, 8 * (f + 1))
                for odd in range(2):
                    last = nc.tensor.matmul(ps[:, 2 + odd, :], wk_sb[:, odd * P:(odd + 1) * P], latT,
                                            start=True, stop=True)
                last.then_inc(qk_ps, 1)

            def project_q(b):
                for odd in range(2):
                    for k in range(KE):
                        last = nc.tensor.matmul(ps[:, 4 + odd, :], wq_sb[:, k, odd * P:(odd + 1) * P], xnT[:, k, :],
                                                start=(k == 0), stop=(k == KE - 1))
                last.then_inc(qk_ps, 1)

            def scores(b, gk):
                g, k = gk // TT, gk % TT
                n = T - P * k
                for two in range(2):
                    u = 2 * gk + two
                    if u >= 2 or later(b):
                        pe.wait_ge(exp_done, 2 * STEPS * b + u - 1)
                    for h in range(2):
                        head = g * HG + 2 * two + h
                        last = nc.tensor.matmul(ps[:, 2 * two + h, 0:n], ks[:, head, k * P:(k + 1) * P],
                                                qs[:, head, k * P:T], start=True, stop=True)
                    last.then_inc(st_ps, 1)

            def weigh(b, gk):
                g, k = gk // TT, gk % TT
                n = T - P * k
                pe.wait_ge(exp_done, 2 * (STEPS * b + gk + 1))
                if k == 0 and (g or later(b)):
                    pe.wait_ge(o_sb, NG * b + g)
                for h in range(HG):
                    last = nc.tensor.matmul(ps[h * COL:h * COL + VW, 4, k * P:T], v_sb[:, k, g * HG + h, :],
                                            probs[:, gk % 2, h, 0:n], start=(k == 0), stop=(k == TT - 1),
                                            skip_group_check=True)
                last.then_inc(av_done, 1)

            def turn_group(b, g):
                pe.wait_ge(o_sb, NG * b + g + 1)
                if g or later(b):
                    pe.wait_ge(on_done, NG * b + g)
                for t in range(TT):
                    last = nc.tensor.transpose(ps[:, 5, t * P:(t + 1) * P], og[:, t * P:(t + 1) * P], id_sb[:])
                last.then_inc(o_ps, 1)

            def attention(b, f_before, p):
                pe.wait_ge(stack_in, STACKS * (b + 1))
                pe.wait_ge(mrow_in[0], 16 * (b + 1))
                pe.wait_ge(v_sbs, b + 1)
                if f_before is not None and later(f_before):
                    pe.wait_ge(w3_used, TT * f_before)
                scores(b, 0)
                for gk in range(STEPS):
                    if gk + 1 == STEPS // 2:
                        pe.wait_ge(mrow_in[1], 16 * (b + 1))
                    if gk + 1 < STEPS:
                        scores(b, gk + 1)
                    weigh(b, gk)
                    if p is not None and gk == 9:
                        turn_x(p)
                    if p is not None and gk == 12:
                        latents(p)
                    if gk % TT == 1 and gk > TT:
                        turn_group(b, gk // TT - 1)
                turn_group(b, NG - 1)

            def products(out_, w, cols, src, tokens, fast, weights_first=True, tiles=None, ready=None):
                tiles = tiles or range(src.shape[1])
                for k in tiles:
                    if ready is not None:
                        pe.wait_ge(ready[0], ready[1] + k + 1)
                    both = (w[:, k, :], src[:, k, :])
                    pairs = list(zip(*map(f16, both))) if fast else [both]
                    for n, (w_k, src_k) in enumerate(pairs):
                        lhs, rhs = (w_k[:, cols], src_k[:, tokens]) if weights_first else (src_k[:, tokens], w_k[:, cols])
                        last = nc.tensor.matmul(out_, lhs, rhs, start=(k == 0 and n == 0),
                                                stop=(k == src.shape[1] - 1 and n == len(pairs) - 1),
                                                skip_group_check=True)
                return last

            def gated_in(b, p, fast):
                pe.wait_ge(x2_done, b + 1)
                for m in range(KF):
                    if m >= 3:
                        pe.wait_ge(gated, 8 * b + m - 2)
                    elif m == 2 and p is not None:
                        pe.wait_ge(lat_sb, p + 1)
                    for w, bank in ((w1_sb, 0), (w2_sb, 1)):
                        last = products(ps[:, L1_BANKS[m % 3] + bank, :], w, slice(m * P, (m + 1) * P),
                                        turned, slice(0, T), fast)
                    last.then_inc(l1_ps, 1)

            def hidden(b, m, w, src, ready, own, done, fast, halves=(0, 1), banks=4):
                if 0 in halves and m >= banks:
                    pe.wait_ge(own, 8 * b + m - banks + 1)
                last = products(ps[:, m % banks, :], w, slice(m * P, (m + 1) * P), src, slice(0, T), fast,
                                tiles=range(halves[0] * KF // 2, (halves[-1] + 1) * KF // 2),
                                ready=(ready, 8 * b) if m == 0 else None)
                if 1 in halves:
                    last.then_inc(done, 1)

            def output(b, fast):
                for tiles in (range(0, KF - 1), range(KF - 1, KF)):
                    for n, t in enumerate(OUT_ORDER):
                        if t == 1:
                            pe.wait_ge(gelu3_done, 8 * (b + 1))
                        last = products(ps[:, t, 0:E], w3_sb, slice(0, E), hid_a, slice(t * P, (t + 1) * P), fast,
                                        weights_first=False, tiles=tiles, ready=(g3_done, 8 * b) if n == 0 else None)
                        if tiles[-1] == KF - 1:
                            last.then_inc(w3_ps, 1)

            def turn_attn(b):
                pe.wait_ge(on_done, NG * (b + 1))
                transposes(on, 4).then_inc(onT_ps, 1)

            def attn_out(b):
                pe.wait_ge(onT_sb, b + 1)
                for t in range(TT):
                    for k in range(KE):
                        last = nc.tensor.matmul(ps[:, 6 + t // 2, (t % 2) * E:(t % 2 + 1) * E],
                                                turned[:, k, t * P:(t + 1) * P], wo_sb[:, k, :],
                                                start=(k == 0), stop=(k == KE - 1))
                last.then_inc(wo_ps, 1)

            def turn_x2(b):
                pe.wait_ge(xn2_ready, TT * (b + 1))
                transposes(on, 6).then_inc(x2T_ps, 1)

            def max_scores(b, h2, tiles):
                pe.wait_ge(stack_in, STACKS * (b + 1))
                for t in tiles:
                    u = TT * h2 + t
                    n = P * (t + 1)
                    if u >= 2 or later(b):
                        pe.wait_ge(mx_used, 32 * b + u - 1)
                    for h in range(2):
                        head = 2 * h2 + h
                        last = nc.tensor.matmul(ps[:, 4 + 2 * (u % 2) + h, 0:n],
                                                qs[0:ROW_MAX, head, t * P:(t + 1) * P], ks[0:ROW_MAX, head, 0:n],
                                                start=True, stop=True)
                    last.then_inc(mx_ps, 1)

            def turn_max(b, half_):
                pe.wait_ge(msplit, 8 * b + 4 * (half_ + 1))
                for t in range(TT):
                    last = nc.tensor.transpose(ps_mt[half_][:, t * P:(t + 1) * P],
                                               ms[:, t].rearrange("p r h -> p (r h)"), idb_sb[:])
                last.then_inc(mT_ps, 1)

            def steps(a, f, p, fast):
                if a is not None:
                    attention(a, f, p)
                elif p is not None:
                    turn_x(p)
                    latents(p)
                if f is not None:
                    if a is None:
                        if later(f):
                            pe.wait_ge(w3_used, TT * f)
                    else:
                        pe.wait_ge(exp_done, 2 * STEPS * (a + 1))
                    gated_in(f, p, fast)
                if a is not None:
                    turn_attn(a)
                if p is not None:
                    project_kv(p, f)
                elif f is not None:
                    pe.wait_ge(gated, 8 * (f + 1))
                if a is not None:
                    attn_out(a)
                if p is not None:
                    project_q(p)
                if p is not None:
                    pe.wait_ge(v_sbs, p + 1)
                for m in range(KF):
                    if a is not None and m == KF - 2:
                        turn_x2(a)
                    if f is not None:
                        if p is not None and m == 2:
                            pe.wait_ge(terms, 8 * p + 4)
                        hidden(f, m, h1_sb, hid_a, g1_done, gelu2_done, l2_ps, fast)
                if p is not None:
                    pe.wait_ge(terms, 8 * (p + 1))
                    max_scores(p, 0, range(0, 1))
                if a is not None:
                    if later(a):
                        pe.wait_ge(x2_done, a + 1)
                    else:
                        pe.wait_ge(x2T_sb, 1)
                if p is not None:
                    max_scores(p, 0, range(1, TT))
                for m in range(KF):
                    for half_ in range(2):
                        if p is not None and m + 1 < KF:
                            max_scores(p, m + 1, range(2 * half_, 2 * half_ + 2))
                        if f is not None:
                            if m < 3:
                                pe.wait_ge(gelu2_done, 8 * f + 5 + m)
                            hidden(f, m, h2_sb, hid_b, g2_done, gelu3_done, l3_ps, fast, (half_,), 3)
                        if p is not None and m % 4 == 3 and half_ == 0:
                            turn_max(p, m // 4)
                if f is not None:
                    output(f, fast)

            pe.wait_ge(sums_clear, 1)
            pe.wait_ge(weights_in, WEIGHT_LOADS * 16)
            schedule(pe, steps, True, lambda: pe.wait_ge(float32_in, 80))


def tables():
    inv = 1.0 / 10000.0 ** (np.arange(0, D, 2, dtype=np.float32) / D)
    ang = np.outer(np.arange(T, dtype=np.float32), inv)
    cos, sin = (np.repeat(f(ang).astype(np.float32).T, H, axis=0) for f in (np.cos, np.sin))
    tile, page = np.arange(T) // P, np.arange(T) // PAGE % 2
    q, k = np.zeros((2, P - ROWS_QK, T), np.float32)
    for t in range(TT):
        q[t] = MASKED * ((tile == t) & (page == 0))
        k[t] = (tile == t) & (page == 1)
    k[TT:TT + 3] = 1.0
    return cos, sin, q, k


def kernel(L0_attn_x, L0_attn_wq, L0_attn_w_down, L0_attn_wk_up, L0_attn_wv_up, L0_attn_wo,
           L0_ffn_w1_w, L0_ffn_w1_s, L0_ffn_w2_w, L0_ffn_w2_s, L0_ffn_h1_w, L0_ffn_h1_s,
           L0_ffn_h2_w, L0_ffn_h2_s, L0_ffn_w3_w, L0_ffn_w3_s):
    import ml_dtypes
    import concourse.bacc as bacc
    from concourse.bass_utils import run_bass_kernel_spmd

    cols = np.arange(E).reshape(H, D // 2, 2).transpose(2, 1, 0).reshape(E)
    cos, sin, qconst, kconst = tables()
    per_tile = lambda s: np.asarray(s).reshape(KF, P).T
    data = dict(
        x=L0_attn_x, wq=np.asarray(L0_attn_wq)[:, cols], wd=L0_attn_w_down,
        wk=np.asarray(L0_attn_wk_up)[:, cols], wv=L0_attn_wv_up, wo=L0_attn_wo,
        w1=np.asarray(L0_ffn_w1_w).T, s1=per_tile(L0_ffn_w1_s), w2=np.asarray(L0_ffn_w2_w).T,
        s2=per_tile(L0_ffn_w2_s), h1=np.asarray(L0_ffn_h1_w).T, sh1=per_tile(L0_ffn_h1_s),
        h2=np.asarray(L0_ffn_h2_w).T, sh2=per_tile(L0_ffn_h2_s), w3=np.asarray(L0_ffn_w3_w).T,
        s3=np.asarray(L0_ffn_w3_s).reshape(1, E), cos=cos, sin=sin,
        qconst=qconst.astype(ml_dtypes.bfloat16), kconst=kconst.astype(ml_dtypes.bfloat16),
        ident=np.eye(P, dtype=np.float32), identb=np.eye(P, dtype=ml_dtypes.bfloat16))
    nc = bacc.Bacc("TRN2", target_bir_lowering=False, num_devices=1)
    arrays = {f"in_{n}": np.ascontiguousarray(a) for n, a in data.items()}
    args = [nc.dram_tensor(n, a.shape, mybir.dt.from_np(a.dtype), kind="ExternalInput").ap()
            for n, a in arrays.items()]
    args.append(nc.dram_tensor("out", (B, T, E), F32, kind="ExternalOutput").ap())
    program(nc, *args)
    return run_bass_kernel_spmd(nc, [arrays], core_ids=[0]).results[0]["out"]
```
